# Optimizing a Trainium2 kernel written in Bass

```python
import numpy as np
import jax
import jax.numpy as jnp

def _softmax(x, axis=-1):
    return jax.nn.softmax(x, axis=axis)

def _gelu(x):
    return jax.nn.gelu(x, approximate=True)

def _silu(x):
    return jax.nn.silu(x)

def _sigmoid(x):
    return jax.nn.sigmoid(x)

def _layernorm(x, axis=-1, eps=1e-05):
    m = jnp.mean(x, axis=axis, keepdims=True)
    v = jnp.var(x, axis=axis, keepdims=True)
    return (x - m) / jnp.sqrt(v + eps)

def _scatter_add(tgt, idx, src, axis=0):
    return tgt.at[idx].add(src)

def _segment_sum(src, seg, n):
    return jax.ops.segment_sum(src, seg, n)
kernel_name = 'mk_flamingo_gated_d1_seqx_r4_367ba1'

def setup_inputs(seed: int=0):
    np.random.seed(seed)
    _w = jnp.asarray

    def _rec_inputs():
        import jax
        import jax.numpy as jnp
        _rk = jax.random.key(seed)
        x = -0.0002928 + 1 * jax.random.normal(jax.random.fold_in(_rk, 1), (32, 128, 256), jnp.float32)
        _lenS = 128 - jax.random.randint(jax.random.fold_in(_rk, 7), (32,), 0, max(1, 128 // 4) + 1, jnp.int32)
        _lenS2 = 128 - jax.random.randint(jax.random.fold_in(_rk, 8), (32,), 0, max(1, 128 // 4) + 1, jnp.int32)
        _ctx_1024P = jax.random.normal(jax.random.fold_in(_rk, 11), (32, 16, 256), jnp.float32)
        _ctx_1024c = jax.random.dirichlet(jax.random.fold_in(_rk, 511), 0.3 * jnp.ones((16,), jnp.float32), (32, 128))
        _ctx_1024t = jnp.einsum('bsk,bkd->bsd', _ctx_1024c, _ctx_1024P)
        _ctx_1024t = _ctx_1024t * jax.lax.rsqrt(jnp.mean(jnp.square(_ctx_1024t)) + 1e-12) * 0.953939
        ctx_1024 = -1.39393e-06 + 0.999914 * (_ctx_1024t + 0.3 * jax.random.normal(jax.random.fold_in(_rk, 611), (32, 128, 256), jnp.float32))
        _g = jax.random.normal(jax.random.fold_in(_rk, 9001), (2, 1), jnp.float32)
        _g = jnp.sign(_g) * jnp.maximum(jnp.abs(_g), 1.0) + (_g == 0) * 1.0
        g_xattn = _g[0]
        g_ffn = _g[1]
        return (x, ctx_1024, g_xattn, g_ffn)
    x, ctx_1024, g_xattn, g_ffn = _rec_inputs()

    def _L0_xattn_setup():
        import jax, jax.numpy as jnp
        import numpy as np
        D_MODEL = 256
        N_HEADS = 16
        D_HEAD = D_MODEL // N_HEADS
        WINDOW = 128

        def _heads(x):
            B, S, _ = x.shape
            return x.reshape(B, S, N_HEADS, D_HEAD).transpose(0, 2, 1, 3)
        key = jax.random.key(seed)
        ks = jax.random.split(key, 11)
        B, S = (1, 1024)
        s = 1.0 / np.sqrt(D_MODEL)
        return {'query': jax.random.normal(ks[0], (B, S, D_MODEL), jnp.float32), 'key': jax.random.normal(ks[1], (B, S, D_MODEL), jnp.float32), 'value': jax.random.normal(ks[2], (B, S, D_MODEL), jnp.float32), 'Wq': jax.random.normal(ks[3], (D_MODEL, D_MODEL), jnp.float32) * s, 'bq': jnp.zeros((D_MODEL,), jnp.float32), 'Wk': jax.random.normal(ks[4], (D_MODEL, D_MODEL), jnp.float32) * s, 'bk': jnp.zeros((D_MODEL,), jnp.float32), 'Wv': jax.random.normal(ks[5], (D_MODEL, D_MODEL), jnp.float32) * s, 'bv': jnp.zeros((D_MODEL,), jnp.float32), 'Wo': jax.random.normal(ks[6], (D_MODEL, D_MODEL), jnp.float32) * s, 'bo': jnp.zeros((D_MODEL,), jnp.float32)}
    _L0_xattn_all = _L0_xattn_setup()
    _L0_xattn_in = {k: v for k, v in _L0_xattn_all.items() if k in ('Wq', 'bq', 'Wk', 'bk', 'Wv', 'bv', 'Wo', 'bo')}
    del _L0_xattn_all

    def _L0_ffn_setup():
        import jax, jax.numpy as jnp
        import numpy as np
        NUM_NOD = 6
        MAX_PREV = 5
        NUM_EDGE = 20
        D = 256
        H = 8
        LN_EPS = 1e-06

        def _layernorm(x, g, b):
            mu = jnp.mean(x, axis=-1, keepdims=True)
            var = jnp.mean(jnp.square(x - mu), axis=-1, keepdims=True)
            return (x - mu) * jax.lax.rsqrt(var + LN_EPS) * g + b

        def _mha(q, k, v, wq, wk, wv, wo):
            B, S, d = q.shape
            dh = d // H
            qh = (q @ wq).reshape(B, S, H, dh)
            kh = (k @ wk).reshape(B, S, H, dh)
            vh = (v @ wv).reshape(B, S, H, dh)
            scores = jnp.einsum('bqhd,bkhd->bhqk', qh, kh) / jnp.sqrt(jnp.asarray(dh, q.dtype))
            attn = jax.nn.softmax(scores, axis=-1)
            ctx = jnp.einsum('bhqk,bkhd->bqhd', attn, vh).reshape(B, S, d)
            return ctx @ wo
        key = jax.random.key(seed)
        ks = jax.random.split(key, 12)
        B, S = (8, 256)
        scale = 1.0 / np.sqrt(D)
        return {'inputs': jax.random.normal(ks[0], (B, S, D), jnp.float32), 'ew': jax.random.uniform(ks[1], (NUM_NOD, 3), jnp.float32), 'act_w': jax.random.uniform(ks[2], (NUM_NOD,), jnp.float32), 'We': jax.random.normal(ks[3], (NUM_EDGE, D, D), jnp.float32) * scale, 'be': jnp.zeros((NUM_EDGE, D), jnp.float32), 'Wq': jax.random.normal(ks[4], (NUM_NOD, D, D), jnp.float32) * scale, 'Wk': jax.random.normal(ks[5], (NUM_NOD, D, D), jnp.float32) * scale, 'Wv': jax.random.normal(ks[6], (NUM_NOD, D, D), jnp.float32) * scale, 'Wo': jax.random.normal(ks[7], (NUM_NOD, D, D), jnp.float32) * scale, 'ln_g': jnp.ones((D,), jnp.float32), 'ln_b': jnp.zeros((D,), jnp.float32)}
    _L0_ffn_all = _L0_ffn_setup()
    _L0_ffn_in = {k: v for k, v in _L0_ffn_all.items() if k in ('ew', 'act_w', 'We', 'be', 'Wq', 'Wk', 'Wv', 'Wo', 'ln_g', 'ln_b')}
    del _L0_ffn_all
    return {'x': x, 'ctx_1024': ctx_1024, 'g_xattn': g_xattn, 'g_ffn': g_ffn, 'L0_xattn_Wq': _L0_xattn_in['Wq'], 'L0_xattn_bq': _L0_xattn_in['bq'], 'L0_xattn_Wk': _L0_xattn_in['Wk'], 'L0_xattn_bk': _L0_xattn_in['bk'], 'L0_xattn_Wv': _L0_xattn_in['Wv'], 'L0_xattn_bv': _L0_xattn_in['bv'], 'L0_xattn_Wo': _L0_xattn_in['Wo'], 'L0_xattn_bo': _L0_xattn_in['bo'], 'L0_ffn_ew': _L0_ffn_in['ew'], 'L0_ffn_act_w': _L0_ffn_in['act_w'], 'L0_ffn_We': _L0_ffn_in['We'], 'L0_ffn_be': _L0_ffn_in['be'], 'L0_ffn_Wq': _L0_ffn_in['Wq'], 'L0_ffn_Wk': _L0_ffn_in['Wk'], 'L0_ffn_Wv': _L0_ffn_in['Wv'], 'L0_ffn_Wo': _L0_ffn_in['Wo'], 'L0_ffn_ln_g': _L0_ffn_in['ln_g'], 'L0_ffn_ln_b': _L0_ffn_in['ln_b']}

def reference(x, ctx_1024, g_xattn, g_ffn, L0_xattn_Wq, L0_xattn_bq, L0_xattn_Wk, L0_xattn_bk, L0_xattn_Wv, L0_xattn_bv, L0_xattn_Wo, L0_xattn_bo, L0_ffn_ew, L0_ffn_act_w, L0_ffn_We, L0_ffn_be, L0_ffn_Wq, L0_ffn_Wk, L0_ffn_Wv, L0_ffn_Wo, L0_ffn_ln_g, L0_ffn_ln_b):
    import jax
    import jax.numpy as jnp

    def _L0_xattn_ref(query, key, value, Wq, bq, Wk, bk, Wv, bv, Wo, bo):
        import jax, jax.numpy as jnp
        import numpy as np
        D_MODEL = 256
        N_HEADS = 16
        D_HEAD = D_MODEL // N_HEADS
        WINDOW = 128

        def _heads(x):
            B, S, _ = x.shape
            return x.reshape(B, S, N_HEADS, D_HEAD).transpose(0, 2, 1, 3)
        B, S, _ = query.shape
        q = _heads(query @ Wq.T + bq)
        k = _heads(key @ Wk.T + bk)
        v = _heads(value @ Wv.T + bv)
        scores = jnp.einsum('bhqd,bhkd->bhqk', q, k) / np.sqrt(D_HEAD).astype(np.float32)
        idx = jnp.arange(S)
        local = jnp.abs(idx[:, None] - idx[None, :]) <= WINDOW // 2
        scores = jnp.where(local[None, None, :, :], scores, -jnp.inf)
        attn = jax.nn.softmax(scores, axis=-1)
        ctx = jnp.einsum('bhqk,bhkd->bhqd', attn, v)
        ctx = ctx.transpose(0, 2, 1, 3).reshape(B, S, D_MODEL)
        return ctx @ Wo.T + bo

    def _L0_ffn_ref(inputs, ew, act_w, We, be, Wq, Wk, Wv, Wo, ln_g, ln_b):
        import jax, jax.numpy as jnp
        import numpy as np
        NUM_NOD = 6
        MAX_PREV = 5
        NUM_EDGE = 20
        D = 256
        H = 8
        LN_EPS = 1e-06

        def _layernorm(x, g, b):
            mu = jnp.mean(x, axis=-1, keepdims=True)
            var = jnp.mean(jnp.square(x - mu), axis=-1, keepdims=True)
            return (x - mu) * jax.lax.rsqrt(var + LN_EPS) * g + b

        def _mha(q, k, v, wq, wk, wv, wo):
            B, S, d = q.shape
            dh = d // H
            qh = (q @ wq).reshape(B, S, H, dh)
            kh = (k @ wk).reshape(B, S, H, dh)
            vh = (v @ wv).reshape(B, S, H, dh)
            scores = jnp.einsum('bqhd,bkhd->bhqk', qh, kh) / jnp.sqrt(jnp.asarray(dh, q.dtype))
            attn = jax.nn.softmax(scores, axis=-1)
            ctx = jnp.einsum('bhqk,bkhd->bqhd', attn, vh).reshape(B, S, d)
            return ctx @ wo
        nodes = {-1: inputs}
        lind = 0
        for c in range(NUM_NOD):
            nsrc = min(c + 1, MAX_PREV)
            snode = c - nsrc
            eq, ek, ev = (lind + nsrc - 1, lind, lind + nsrc // 2)
            in_q, in_k, in_v = (c - 1, snode, snode + nsrc // 2)
            q = ew[c, 0] * (nodes[in_q] @ We[eq] + be[eq])
            k = ew[c, 1] * (nodes[in_k] @ We[ek] + be[ek])
            v = ew[c, 2] * (nodes[in_v] @ We[ev] + be[ev])
            o = _mha(q, k, v, Wq[c], Wk[c], Wv[c], Wo[c])
            nodes[c] = act_w[c] * o + q
            lind += nsrc
        out = nodes[NUM_NOD - 1]
        return _layernorm(out, ln_g, ln_b)
    x = x + jnp.tanh(g_xattn[0]) * _L0_xattn_ref(_layernorm(x, axis=-1), ctx_1024, ctx_1024, L0_xattn_Wq, L0_xattn_bq, L0_xattn_Wk, L0_xattn_bk, L0_xattn_Wv, L0_xattn_bv, L0_xattn_Wo, L0_xattn_bo)
    x = x + jnp.tanh(g_ffn[0]) * _L0_ffn_ref(_layernorm(x, axis=-1), L0_ffn_ew, L0_ffn_act_w, L0_ffn_We, L0_ffn_be, L0_ffn_Wq, L0_ffn_Wk, L0_ffn_Wv, L0_ffn_Wo, L0_ffn_ln_g, L0_ffn_ln_b)
    return x

_drawn_inputs = setup_inputs


def setup_inputs(seed=0):
    import zlib

    import numpy as np

    out = dict(_drawn_inputs(seed))
    spreads = {'L0_xattn_bq': (0.0, 0.593),
     'L0_xattn_bk': (0.0, 2.0),
     'L0_xattn_bv': (0.0, 0.1),
     'L0_xattn_bo': (0.0, 0.1),
     'L0_ffn_be': (0.0, 0.1),
     'L0_ffn_ln_g': (1.0, 0.2),
     'L0_ffn_ln_b': (0.0, 0.1)}
    factors = {'L0_ffn_Wq': 197.381, 'L0_ffn_Wk': 194.938}
    for name, (base, spread) in spreads.items():
        noise = np.random.default_rng([zlib.crc32(name.encode()), seed]).standard_normal(out[name].shape)
        drawn = base * np.exp(spread * noise) if base else spread * noise
        out[name] = jnp.asarray(drawn.astype(out[name].dtype))
    for name, factor in factors.items():
        out[name] = (out[name] * factor).astype(out[name].dtype)
    return out
```

```python
from collections import namedtuple
from contextlib import ExitStack

import numpy as np

import concourse.bass as bass
from concourse import mybir

P = 128
D = 256
SEQ = 128
BATCH = 32
PAIR = 2
TOK = PAIR * SEQ
CHAINS = 2
ITERS = BATCH // (PAIR * CHAINS)
KT = D // P
NODES = 6
MAX_PREV = 5
EDGES = 20
A_HEADS, A_DH = 16, 16
N_HEADS, N_DH = 8, 32
WINDOW = 128
G = 4
EPS_PRE = 1e-5
EPS_OUT = 1e-6
MASKED = -1e30

F32 = mybir.dt.float32
F32R = mybir.dt.float32r
ALU = mybir.AluOpType
ACT = mybir.ActivationFunctionType
AX_X = mybir.AxisListType.X

WQ, WQH, WK, WV, WO = range(5)
AQ, AK, AV, AO = range(4)

Step = namedtuple("Step", "kind z stage part")


def wiring():
    out, first = [], 0
    for c in range(NODES):
        n = min(c + 1, MAX_PREV)
        src = c - n
        out.append(dict(eq=first + n - 1, ek=first, ev=first + n // 2, q=c - 1, k=src, v=src + n // 2))
        first += n
    return out


WIRES = wiring()
STAGES = 2 + NODES


def projections(z, s):
    if s == 0:
        return [Step("norm_in", z, s, 0), Step("turn", z, s, 0), Step("k", z, s, 0), Step("v", z, s, 0),
                Step("q", z, s, 0)]
    if s == 1:
        return [Step("k", z, s, 0)]
    if s == 2:
        return [Step("cross_out", z, s, 0), Step("norm_x1", z, s, 0), Step("turn", z, s, 0),
                Step("q", z, s, 0), Step("k", z, s, 0), Step("k", z, s, 1), Step("qh", z, s, 0), Step("v", z, s, 0)]
    if s < STAGES:
        return [Step("k", z, s, 0), Step("node_out", z, s, 0), Step("k", z, s, 1), Step("q", z, s, 0),
                Step("v", z, s, 0), Step("qh", z, s, 0)]
    return [Step("node_out", z, s, 0), Step("turn_back", z, s, 0), Step("finish", z, s, 0)]


def attention(z, s):
    sc, nm, tr, pv = ([Step(k, z, s, u) for u in range(4)] for k in ("scores", "scale", "turn_p", "mix"))
    return [sc[0], None, sc[1], None, nm[0], tr[0], None, nm[1], sc[2], mix_of(pv, 0), tr[1], None, sc[3], nm[2],
            mix_of(pv, 1), tr[2], None, nm[3], mix_of(pv, 2), tr[3], None, mix_of(pv, 3)]


def mix_of(pv, u):
    return pv[u]


def merged(att, proj):
    out, left = [], list(proj)
    for x in att:
        if x is not None:
            out.append(x)
        elif left:
            out.append(left.pop(0))
            while left and left[0].kind in ("norm_x1", "norm_in", "finish"):
                out.append(left.pop(0))
    return out + left


def plan():
    steps = projections(0, 0)
    for s in range(STAGES):
        steps += merged(attention(0, s), projections(1, s))
        steps += merged(attention(1, s), projections(0, s + 1))
    return steps + projections(1, STAGES)


STEPS = plan()

SIGNALS = {
    "projected": ("turn", "k", "v", "q", "qh", "node_out", "cross_out", "turn_back"),
    "act_took": ("turn", "v", "q", "qh"),
    "dve_took": ("k", "node_out", "cross_out"),
    "var_ready": ("norm_in", "norm_x1", "finish"),
    "normed": ("norm_in", "norm_x1", "finish"),
    "scored": ("scores",),
    "max_ready": ("scores",),
    "exp_done": ("scores",),
    "inv_ready": ("scale",),
    "scaled": ("scale",),
    "turned_p": ("turn_p",),
    "pt_ready": ("turn_p",),
    "mixed": ("mix",),
}


def ordinals():
    when, total = {}, {}
    for name, kinds in SIGNALS.items():
        n = 0
        for st in STEPS:
            if st.kind in kinds:
                n += 1
                when[name, st] = n
        total[name] = n
    return when, total


WHEN, TOTAL = ordinals()
PROJ = [st for st in STEPS if st.kind in SIGNALS["projected"]]
UNITS = [st for st in STEPS if st.kind == "scores"]


def due(name, it, st):
    return it * TOTAL[name] + WHEN[name, st]


def unit_of(st):
    if st.stage < 2:
        return st.part // 2, st.stage, G * (st.part % 2)
    return st.part % 2, st.part // 2, G * (st.part // 2)


def out_banks():
    out, n = {}, 0
    for st in STEPS:
        if st.kind == "mix":
            per = 4 if st.stage < 2 else 2
            out[st] = (n, st.part % per == 0, st.part % per == per - 1)
            n += st.part % per == per - 1
    return out, n


OUT_OF, OUTS = out_banks()


def out_due(it, z, s, half):
    last = [OUT_OF[st] for st in OUT_OF if st.z == z and st.stage == s and OUT_OF[st][2]]
    return it * OUTS + (last[half if s >= 2 else 0][0] + 1)


def build(nc, a):
    ctx = ExitStack()
    with ctx:
        def sb(name, shape, dt=F32):
            return ctx.enter_context(nc.sbuf_tensor(name, shape, dt))

        def sem(name):
            return ctx.enter_context(nc.semaphore(name))

        w_cross = sb("w_cross", [P, 4, KT, D])
        w_node = sb("w_node", [P, NODES, 5, KT, D])
        b_cross = sb("b_cross", [P, 3, KT])
        b_node = sb("b_node", [P, NODES, 3, KT])
        be_col = sb("be_col", [P, EDGES, KT])
        rows = sb("rows", [P, 3, D])
        scalars = sb("scalars", [P, 3 * NODES + NODES + 2])
        gates = sb("gates", [P, 2])
        ident = sb("ident", [P, P])
        ident_r = sb("ident_r", [P, P], F32R)
        band_f = sb("band_f", [P, P])
        band_r = sb("band_r", [P, G, P], F32R)
        own = sb("own", [P, 8 + 4])
        idle = sb("idle", [P, 1])
        half_neg = sb("half_neg", [P, PAIR])
        stage_t = sb("stage_t", [P, 2, KT, D])
        stage_w = sb("stage_w", [P, 2, KT, D])

        def per_chain(name, shape, dt=F32):
            return [sb(f"{name}{z}", shape, dt) for z in range(CHAINS)]

        x_in = per_chain("x_in", [P, PAIR, D])
        x_bias = per_chain("x_bias", [P, PAIR, D])
        x1 = per_chain("x1", [P, PAIR, D])
        normed_x = per_chain("normed_x", [P, PAIR, D])
        ctx_t = per_chain("ctx_t", [P, KT, TOK])
        stats = per_chain("stats", [P, PAIR, 6])
        moments = per_chain("moments", [P, PAIR, 2])
        var_eps = per_chain("var_eps", [P, PAIR])
        rstd = per_chain("rstd", [P, PAIR])
        SLOT = {-2: 3, -1: 0, 0: 1, 1: 2, 2: 3, 3: 4, 4: 0, 5: 2}
        node_t = per_chain("node_t", [P, 5, KT, TOK])
        q_t = per_chain("q_t", [P, KT, TOK])
        qh_t = per_chain("qh_t", [P, KT, TOK])
        k_blk = per_chain("k_blk", [P, 8, TOK])
        v_pad = per_chain("v_pad", [P, PAIR * A_HEADS // 2, 64])
        v_row = per_chain("v_row", [P, PAIR, D])
        o_t = per_chain("o_t", [P, KT, TOK])
        probs = sb("probs", [P, 3, G, SEQ])
        probs_t = sb("probs_t", [P, 2, G, SEQ])
        neg_max = sb("neg_max", [P, 4, G])
        row_sum = sb("row_sum", [P, 4, G])
        inv_sum = sb("inv_sum", [P, 4, G])

        def bank(name):
            return ctx.enter_context(nc.psum_tensor(name, [P, 512], F32))

        ps_proj = [bank(f"ps_proj{i}") for i in range(2)]
        ps_score = [bank(f"ps_score{i}") for i in range(2)]
        ps_turn = [bank(f"ps_turn{i}") for i in range(2)]
        ps_out = [bank(f"ps_out{i}") for i in range(2)]

        s = {name: sem(name) for name in SIGNALS}
        out_taken = sem("out_taken")
        x_loaded = [sem(f"x_loaded{z}") for z in range(CHAINS)]
        ctx_loaded = [sem(f"ctx_loaded{z}") for z in range(CHAINS)]
        x_used = sem("x_used")
        rstd_ready = sem("rstd_ready")
        x1_used = sem("x1_used")
        result_ready = sem("result_ready")
        pool_step = sem("pool_step")
        dve_step = sem("dve_step")
        stored = [sem(f"stored{z}") for z in range(CHAINS)]
        consts_in = sem("consts_in")
        weights_in = sem("weights_in")
        stage_in = [sem(f"stage_in{i}") for i in range(2)]
        gates_ready = sem("gates_ready")
        prep_act = sem("prep_act")
        prep_dve = sem("prep_dve")
        prep_pe = sem("prep_pe")
        zeroed = sem("zeroed")

        block = ctx.enter_context(nc.Block())

        x_v = a["x"].rearrange("(i z b) t d -> i z t b d", z=CHAINS, b=PAIR)
        ctx_v = a["ctx_t"]
        out_v = a["out"].rearrange("(i z b) t d -> i z t b d", z=CHAINS, b=PAIR)

        PRODUCTS = [(c, w, WIRES[c][e]) for c in range(NODES) for w, e in ((WK, "ek"), (WV, "ev"))]
        N_CONST = 7
        N_WEIGHT = 1 + 3 * NODES

        def ew(c, i):
            return scalars[:, 3 * c + i:3 * c + i + 1]

        def act_w(c):
            return scalars[:, 3 * NODES + c:3 * NODES + c + 1]

        def bcast(ap, n, m):
            return ap.rearrange("p (n o) -> p n o", o=1).to_broadcast([P, n, m])

        def on_all(dram, n):
            return dram.rearrange("(o n) -> o n", o=1).to_broadcast([P, n])

        @block.sync
        def _(sp):
            def load_x(it, z):
                sp.dma_start(x_in[z][:], x_v[it, z]).then_inc(x_loaded[z], 16)

            def load_ctx(it, z):
                sp.dma_start(ctx_t[z][:], ctx_v[it, z]).then_inc(ctx_loaded[z], 16)

            sp.dma_start(scalars[:, 0:3 * NODES], on_all(a["ew"], 3 * NODES)).then_inc(consts_in, 16)
            sp.dma_start(scalars[:, 3 * NODES:4 * NODES], on_all(a["act_w"], NODES)).then_inc(consts_in, 16)
            sp.dma_start(scalars[:, 4 * NODES:4 * NODES + 2], on_all(a["gates"], 2)).then_inc(consts_in, 16)
            for i, name in enumerate(("bo", "ln_g", "ln_b")):
                sp.dma_start(rows[:, i, :], on_all(a[name], D)).then_inc(consts_in, 16)
            sp.dma_start(b_cross[:], a["b_cross"]).then_inc(consts_in, 16)
            sp.dma_start(be_col[:], a["be_col"]).then_inc(consts_in, 16)
            sp.dma_start(ident[:], a["ident"]).then_inc(consts_in, 16)
            sp.dma_start(band_f[:], a["band"]).then_inc(consts_in, 16)
            sp.dma_start(own[:], a["own"]).then_inc(consts_in, 16)
            load_x(0, 0)
            load_x(0, 1)
            sp.dma_start(w_cross[:], a["w_cross"]).then_inc(weights_in, 16)
            load_ctx(0, 0)
            load_ctx(0, 1)
            for n, (c, w, e) in enumerate(PRODUCTS):
                if w == WK:
                    for place, src in ((WQ, a["we"][WIRES[c]["eq"]]), (WQH, a["wq"][c]), (WO, a["wo"][c])):
                        sp.dma_start(w_node[:, c, place], src).then_inc(weights_in, 16)
                if n >= 2:
                    sp.wait_ge(prep_pe, n - 1)
                sp.dma_start(stage_t[:, n % 2], a["we_t"][e]).then_inc(stage_in[n % 2], 16)
                sp.dma_start(stage_w[:, n % 2], a["wk" if w == WK else "wv"][c]).then_inc(stage_in[n % 2], 16)

            def store(it, z):
                sp.wait_ge(result_ready, it * CHAINS + z + 1)
                sp.dma_start(out_v[it, z], normed_x[z][:]).then_inc(stored[z], 16)

            with sp.Fori(0, ITERS - 1) as it:
                for z in range(CHAINS):
                    sp.wait_ge(x_used, it * CHAINS + z + 1)
                    load_x(it + 1, z)
                for z in range(CHAINS):
                    sp.wait_ge(s["projected"], due("projected", it, Step("k", z, 1, 0)))
                    load_ctx(it + 1, z)
                for z in range(CHAINS):
                    store(it, z)
            for z in range(CHAINS):
                store(ITERS - 1, z)
                sp.wait_ge(stored[z], 16 * ITERS)

        @block.gpsimd
        def _(pool):
            for z in range(CHAINS):
                nc.gpsimd.memset(v_pad[z][:], 0.0).then_inc(zeroed, 1)
            nc.gpsimd.memset(half_neg[:], -0.5).then_inc(zeroed, 1)
            pool.wait_ge(zeroed, 3)
            pool.wait_ge(prep_dve, 3)
            steps_per_it = 2 * CHAINS

            def root(it, st):
                pool.wait_ge(s["var_ready"], due("var_ready", it, st))
                nc.gpsimd.tensor_tensor(rstd[st.z][:], var_eps[st.z][:], half_neg[:], ALU.pow).then_inc(rstd_ready, 1)

            with pool.Fori(0, ITERS) as it:
                for st in STEPS:
                    z = st.z
                    both = [P, PAIR, D]
                    if st.kind == "norm_in":
                        root(it, st)
                        pool.wait_ge(s["normed"], due("normed", it, st))
                        pool.wait_ge(result_ready, it * CHAINS)
                        nc.gpsimd.tensor_tensor(x_bias[z][:], x_in[z][:],
                                                rows[:, 0:1, :].to_broadcast(both), ALU.add).then_inc(x_used, 1)
                    elif st.kind == "norm_x1":
                        root(it, st)
                        pool.wait_ge(s["dve_took"], due("dve_took", it, Step("cross_out", z, 2, 0)))
                        nc.gpsimd.tensor_tensor(x_bias[z][:], x1[z][:],
                                                rows[:, 2:3, :].to_broadcast(both), ALU.add).then_inc(x1_used, 1)
                    elif st.kind == "finish":
                        root(it, st)
                        pool.wait_ge(s["normed"], due("normed", it, st))
                        nc.gpsimd.tensor_tensor(normed_x[z][:], normed_x[z][:],
                                                rows[:, 1:2, :].to_broadcast(both), ALU.mult).then_inc(pool_step, 1)
                        pool.wait_ge(pool_step, it * CHAINS + z + 1)
                        pool.wait_ge(x1_used, it * CHAINS + z + 1)
                        nc.gpsimd.tensor_tensor(normed_x[z][:], normed_x[z][:], x_bias[z][:],
                                                ALU.add).then_inc(result_ready, 1)
                    elif st.kind == "scale":
                        u = WHEN["scaled", st] - 1
                        pool.wait_ge(s["inv_ready"], due("inv_ready", it, st))
                        p = probs[:, u % 3]
                        nc.gpsimd.tensor_tensor(p, p, bcast(inv_sum[:, u % 4, :], G, SEQ),
                                                ALU.mult).then_inc(s["scaled"], 1)

        @block.scalar
        def _(act):
            act.wait_ge(consts_in, 11 * 16)
            nc.scalar.activation(gates[:], scalars[:, 4 * NODES:4 * NODES + 2], ACT.Tanh).then_inc(gates_ready, 1)
            for n, (c, w, e) in enumerate(PRODUCTS):
                act.wait_ge(prep_pe, n + 1)
                i = 1 if w == WK else 2
                nc.scalar.activation(w_node[:, c, w].rearrange("p k d -> p (k d)"), ps_proj[n % 2][:], ACT.Copy,
                                     scale=ew(c, i)).then_inc(prep_act, 1)
                nc.scalar.activation(b_node[:, c, i], ps_score[n % 2][:, 0:KT], ACT.Copy,
                                     scale=ew(c, i)).then_inc(prep_act, 1)

            def take(it, st, bias, out):
                ps = ps_proj[(WHEN["projected", st] - 1) % 2]
                for h in range(KT):
                    last = nc.scalar.activation(out[:, h, :], ps[:, h * TOK:(h + 1) * TOK], ACT.Identity,
                                                bias=bias[:, h:h + 1])
                last.then_inc(s["act_took"], 1)

            with act.Fori(0, ITERS) as it:
                for st in STEPS:
                    z, c = st.z, st.stage - 2
                    if st.kind in SIGNALS["act_took"]:
                        act.wait_ge(s["projected"], due("projected", it, st))
                        ps = ps_proj[(WHEN["projected", st] - 1) % 2]
                    if st.kind == "turn":
                        slot = 3 if st.stage == 0 else 0
                        nc.scalar.activation(node_t[z][:, slot].rearrange("p k t -> p (k t)"), ps[:],
                                             ACT.Copy).then_inc(s["act_took"], 1)
                    elif st.kind == "q" and st.stage == 0:
                        take(it, st, b_cross[:, 0], qh_t[z])
                    elif st.kind == "q":
                        take(it, st, b_node[:, c, 0], q_t[z])
                    elif st.kind == "qh":
                        nc.scalar.activation(qh_t[z][:].rearrange("p k t -> p (k t)"), ps[:],
                                             ACT.Copy).then_inc(s["act_took"], 1)
                    elif st.kind == "v" and st.stage == 0:
                        src = ps[:].rearrange("p (g e d) -> p g e d", e=2, d=A_DH)
                        nc.scalar.activation(v_pad[z][:, :, 0:A_DH], src[:, :, 0, :], ACT.Copy)
                        nc.scalar.activation(v_pad[z][:, :, 48:64], src[:, :, 1, :],
                                             ACT.Copy).then_inc(s["act_took"], 1)
                    elif st.kind == "v":
                        nc.scalar.activation(v_row[z][:].rearrange("p b d -> p (b d)"), ps[:],
                                             ACT.Copy).then_inc(s["act_took"], 1)
                    elif st.kind == "scores":
                        u = WHEN["scored", st] - 1
                        act.wait_ge(s["max_ready"], due("max_ready", it, st))
                        for j in range(G):
                            last = nc.scalar.activation(
                                probs[:, u % 3, j, :], ps_score[u % 2][:, j * SEQ:(j + 1) * SEQ], ACT.Exp,
                                bias=neg_max[:, u % 4, j:j + 1], accum_out=row_sum[:, u % 4, j:j + 1])
                        last.then_inc(s["exp_done"], 1)
                    elif st.kind == "mix" and OUT_OF[st][2]:
                        act.wait_ge(s["mixed"], due("mixed", it, st))
                        half = unit_of(st)[1]
                        bias = b_cross[:, 2] if st.stage < 2 else b_node[:, c, 2]
                        nc.scalar.activation(o_t[z][:, half, :], ps_out[OUT_OF[st][0] % 2][:, 0:TOK], ACT.Identity,
                                             bias=bias[:, half:half + 1]).then_inc(out_taken, 1)

        @block.vector
        def _(dve):
            dve.wait_ge(consts_in, 11 * 16)
            nc.vector.tensor_copy(ident_r[:], ident[:]).then_inc(prep_dve, 1)
            nc.vector.tensor_copy(band_r[:], band_f[:].rearrange("p (o k) -> p o k", o=1).to_broadcast([P, G, P]))\
                .then_inc(prep_dve, 1)
            dve.wait_ge(gates_ready, 1)
            nc.vector.tensor_scalar(rows[:, 0, :], rows[:, 0, :], gates[:, 0:1], None, ALU.mult)
            nc.vector.tensor_scalar(rows[:, 1:3, :], rows[:, 1:3, :], gates[:, 1:2], None, ALU.mult)\
                .then_inc(prep_dve, 1)
            nc.vector.tensor_scalar(b_cross[:, 0], b_cross[:, 0], A_DH ** -0.5, None, ALU.mult)
            for c in range(NODES):
                nc.vector.tensor_scalar(b_node[:, c, 0], be_col[:, WIRES[c]["eq"]], ew(c, 0), None, ALU.mult)
            dve.wait_ge(weights_in, 16 * N_WEIGHT)
            nc.vector.tensor_scalar(w_cross[:, AQ], w_cross[:, AQ], A_DH ** -0.5, None, ALU.mult)
            nc.vector.tensor_scalar(w_cross[:, AO], w_cross[:, AO], gates[:, 0:1], None, ALU.mult)
            for c in range(NODES):
                nc.vector.tensor_scalar(w_node[:, c, WQ], w_node[:, c, WQ], ew(c, 0), None, ALU.mult)
                nc.vector.tensor_scalar(w_node[:, c, WQH], w_node[:, c, WQH], N_DH ** -0.5, None, ALU.mult)
                last = nc.vector.tensor_scalar(w_node[:, c, WO], w_node[:, c, WO], act_w(c), None, ALU.mult)
            last.then_inc(prep_dve, 1)

            NORMS = TOTAL["normed"]

            def moments_of(it, st, rows_in, eps):
                z = st.z
                n = it * (2 * NORMS) + 2 * (WHEN["normed", st] - 1)
                for b in range(PAIR):
                    last = nc.vector.bn_stats(stats[z][:, b, :], rows_in[b])
                last.then_inc(dve_step, 1)
                dve.wait_ge(dve_step, n + 1)
                nc.vector.memset(idle[:], 0.0)
                for b in range(PAIR):
                    last = nc.vector.bn_aggr(moments[z][:, b, :], stats[z][:, b, :])
                last.then_inc(dve_step, 1)
                dve.wait_ge(dve_step, n + 2)
                nc.vector.tensor_scalar(var_eps[z][:], moments[z][:, :, 1], eps, None,
                                        ALU.add).then_inc(s["var_ready"], 1)

            def normalize(it, st, rows_in):
                z = st.z
                dve.wait_ge(rstd_ready, due("var_ready", it, st))
                for b in range(PAIR):
                    last = nc.vector.tensor_scalar(normed_x[z][:, b, :], rows_in[b], moments[z][:, b, 0:1],
                                                   rstd[z][:, b:b + 1], ALU.subtract, ALU.mult)
                last.then_inc(s["normed"], 1)

            with dve.Fori(0, ITERS) as it:
                for st in STEPS:
                    z, c = st.z, st.stage - 2
                    if st.kind in ("k", "node_out", "cross_out"):
                        dve.wait_ge(s["projected"], due("projected", it, st))
                        ps = ps_proj[(WHEN["projected", st] - 1) % 2]
                    if st.kind == "norm_in":
                        dve.wait_ge(x_loaded[z], it * 16 + 16)
                        dve.wait_ge(stored[z], it * 16)
                        x_rows = [x_in[z][:, b, :] for b in range(PAIR)]
                        moments_of(it, st, x_rows, EPS_PRE)
                        normalize(it, st, x_rows)
                    elif st.kind == "cross_out":
                        dve.wait_ge(x_used, it * CHAINS + z + 1)
                        nc.vector.tensor_tensor(x1[z][:].rearrange("p b d -> p (b d)"), ps[:],
                                                x_bias[z][:].rearrange("p b d -> p (b d)"),
                                                ALU.add).then_inc(s["dve_took"], 1)
                    elif st.kind == "norm_x1":
                        dve.wait_ge(s["dve_took"], due("dve_took", it, Step("cross_out", z, 2, 0)))
                        x_rows = [x1[z][:, b, :] for b in range(PAIR)]
                        moments_of(it, st, x_rows, EPS_PRE)
                        normalize(it, st, x_rows)
                    elif st.kind == "finish":
                        back = Step("turn_back", z, st.stage, 0)
                        dve.wait_ge(s["projected"], due("projected", it, back))
                        ps = ps_proj[(WHEN["projected", back] - 1) % 2]
                        n_rows = [ps[:, b * D:(b + 1) * D] for b in range(PAIR)]
                        moments_of(it, st, n_rows, EPS_OUT)
                        normalize(it, st, n_rows)
                    elif st.kind == "k":
                        n, place = (8, 0) if st.stage < 2 else (4, 4 * st.part)
                        half = st.stage if st.stage < 2 else st.part
                        mask = own[:, 0:8] if st.stage < 2 else own[:, 8:12]
                        bias = b_cross[:, 1] if st.stage < 2 else b_node[:, c, 1]
                        keys = ps[:, 0:TOK].rearrange("p (o t) -> p o t", o=1).to_broadcast([P, n, TOK])
                        nc.vector.scalar_tensor_tensor(
                            out=k_blk[z][:, place:place + n, :], in0=keys, scalar=bias[:, half:half + 1],
                            in1=bcast(mask, n, TOK), op0=ALU.add, op1=ALU.mult).then_inc(s["dve_took"], 1)
                    elif st.kind == "node_out":
                        nc.vector.tensor_tensor(node_t[z][:, SLOT[c - 1]].rearrange("p k t -> p (k t)"), ps[:],
                                                q_t[z][:].rearrange("p k t -> p (k t)"),
                                                ALU.add).then_inc(s["dve_took"], 1)
                    elif st.kind == "scores":
                        u = WHEN["scored", st] - 1
                        dve.wait_ge(s["scored"], due("scored", it, st))
                        nc.vector.tensor_reduce(neg_max[:, u % 4, :],
                                                ps_score[u % 2][:].rearrange("p (h k) -> p h k", h=G),
                                                AX_X, ALU.max, negate=True).then_inc(s["max_ready"], 1)
                    elif st.kind == "scale":
                        u = WHEN["scaled", st] - 1
                        dve.wait_ge(s["exp_done"], due("exp_done", it, UNITS[u]))
                        nc.vector.reciprocal(inv_sum[:, u % 4, :], row_sum[:, u % 4, :]).then_inc(s["inv_ready"], 1)
                    elif st.kind == "turn_p":
                        u = WHEN["turned_p", st] - 1
                        dve.wait_ge(s["turned_p"], due("turned_p", it, st))
                        nc.vector.tensor_copy(probs_t[:, u % 2].rearrange("p h q -> p (h q)"),
                                              ps_turn[u % 2][:]).then_inc(s["pt_ready"], 1)

        @block.tensor
        def _(pe):
            def project(ps, col, w, src, half):
                for k in range(KT):
                    last = nc.tensor.matmul(ps[:, col:col + TOK], w[:, k, half * P:(half + 1) * P], src[:, k, :],
                                            start=(k == 0), stop=(k == KT - 1))
                return last

            def project_rows(ps, w, src):
                for b in range(PAIR):
                    for k in range(KT):
                        last = nc.tensor.matmul(ps[:, b * D:(b + 1) * D], src[:, k, b * SEQ:(b + 1) * SEQ], w[:, k, :],
                                                start=(k == 0), stop=(k == KT - 1))
                return last

            pe.wait_ge(consts_in, 11 * 16)
            for n, (c, w, e) in enumerate(PRODUCTS):
                pe.wait_ge(stage_in[n % 2], 32 * (n // 2 + 1))
                if n >= 2:
                    pe.wait_ge(prep_act, 2 * (n - 1))
                lhs, rhs = stage_t[:, n % 2], stage_w[:, n % 2]
                for h in range(KT):
                    for k in range(KT):
                        nc.tensor.matmul(ps_score[n % 2][:, h:h + 1], rhs[:, k, h * P:(h + 1) * P],
                                         be_col[:, e, k:k + 1], start=(k == 0), stop=(k == KT - 1))
                for h in range(KT):
                    for k in range(KT):
                        last = nc.tensor.matmul(ps_proj[n % 2][:, h * D:(h + 1) * D], lhs[:, k, h * P:(h + 1) * P],
                                                rhs[:, k, :], start=(k == 0), stop=(k == KT - 1))
                last.then_inc(prep_pe, 1)
            pe.wait_ge(prep_act, 2 * len(PRODUCTS))
            pe.wait_ge(prep_dve, 4)
            pe.wait_ge(zeroed, 3)

            def bank_for(it, st):
                n = WHEN["projected", st] - 1
                if n < 2:
                    pe.wait_ge(s["act_took"], it * TOTAL["act_took"])
                    pe.wait_ge(s["dve_took"], it * TOTAL["dve_took"])
                    pe.wait_ge(s["normed"], it * TOTAL["normed"])
                else:
                    before = PROJ[n - 2]
                    if before.kind == "turn_back":
                        pe.wait_ge(s["normed"], due("normed", it, Step("finish", before.z, STAGES, 0)))
                    else:
                        name = "act_took" if before.kind in SIGNALS["act_took"] else "dve_took"
                        pe.wait_ge(s[name], due(name, it, before))
                return ps_proj[n % 2]

            def node_ready(it, z, n):
                if n == -1:
                    pe.wait_ge(s["act_took"], due("act_took", it, Step("turn", z, 2, 0)))
                else:
                    pe.wait_ge(s["dve_took"], due("dve_took", it, Step("node_out", z, n + 3, 0)))
                return node_t[z][:, SLOT[n]]

            with pe.Fori(0, ITERS) as it:
                for st in STEPS:
                    z, c = st.z, st.stage - 2
                    ps = bank_for(it, st) if st.kind in SIGNALS["projected"] else None
                    if st.kind == "turn":
                        name = "norm_in" if st.stage == 0 else "norm_x1"
                        pe.wait_ge(s["normed"], due("normed", it, Step(name, z, st.stage, 0)))
                        for k in range(KT):
                            for b in range(PAIR):
                                last = nc.tensor.transpose(ps[:, (k * PAIR + b) * P:(k * PAIR + b + 1) * P],
                                                           normed_x[z][:, b, k * P:(k + 1) * P], ident[:])
                        last.then_inc(s["projected"], 1)
                    elif st.kind == "turn_back":
                        last_node = node_ready(it, z, NODES - 1)
                        for b in range(PAIR):
                            for k in range(KT):
                                last = nc.tensor.transpose(ps[:, (b * KT + k) * P:(b * KT + k + 1) * P],
                                                           last_node[:, k, b * SEQ:(b + 1) * SEQ], ident[:])
                        last.then_inc(s["projected"], 1)
                    elif st.kind == "k" and st.stage < 2:
                        pe.wait_ge(ctx_loaded[z], it * 16 + 16)
                        project(ps, 0, w_cross[:, AK], ctx_t[z], st.stage).then_inc(s["projected"], 1)
                    elif st.kind == "k":
                        project(ps, 0, w_node[:, c, WK], node_ready(it, z, WIRES[c]["k"]), st.part)\
                            .then_inc(s["projected"], 1)
                    elif st.kind == "v" and st.stage == 0:
                        pe.wait_ge(ctx_loaded[z], it * 16 + 16)
                        project_rows(ps, w_cross[:, AV], ctx_t[z]).then_inc(s["projected"], 1)
                    elif st.kind == "v":
                        project_rows(ps, w_node[:, c, WV], node_ready(it, z, WIRES[c]["v"]))\
                            .then_inc(s["projected"], 1)
                    elif st.kind == "q":
                        if st.stage == 0:
                            pe.wait_ge(s["act_took"], due("act_took", it, Step("turn", z, 0, 0)))
                            w, src = w_cross[:, AQ], node_t[z][:, 3]
                        else:
                            w, src = w_node[:, c, WQ], node_ready(it, z, WIRES[c]["q"])
                        project(ps, 0, w, src, 0)
                        project(ps, TOK, w, src, 1).then_inc(s["projected"], 1)
                    elif st.kind == "qh":
                        pe.wait_ge(s["act_took"], due("act_took", it, Step("q", z, st.stage, 0)))
                        project(ps, 0, w_node[:, c, WQH], q_t[z], 0)
                        project(ps, TOK, w_node[:, c, WQH], q_t[z], 1).then_inc(s["projected"], 1)
                    elif st.kind == "cross_out":
                        pe.wait_ge(out_taken, out_due(it, z, 1, 0))
                        project_rows(ps, w_cross[:, AO], o_t[z]).then_inc(s["projected"], 1)
                    elif st.kind == "node_out":
                        pe.wait_ge(out_taken, out_due(it, z, st.stage - 1, 1))
                        project(ps, 0, w_node[:, c - 1, WO], o_t[z], 0)
                        project(ps, TOK, w_node[:, c - 1, WO], o_t[z], 1).then_inc(s["projected"], 1)
                    elif st.kind == "scores":
                        u = WHEN["scored", st] - 1
                        b, half, place = unit_of(st)
                        if u < 2:
                            pe.wait_ge(s["exp_done"], it * TOTAL["exp_done"])
                        else:
                            pe.wait_ge(s["exp_done"], due("exp_done", it, UNITS[u - 2]))
                        if st.stage < 2:
                            pe.wait_ge(s["act_took"], due("act_took", it, Step("q", z, 0, 0)))
                            pe.wait_ge(s["dve_took"], due("dve_took", it, Step("k", z, st.stage, 0)))
                            nc.tensor.matmul(ps_score[u % 2][:], ident_r[:], band_r[:].rearrange("p h k -> p (h k)"),
                                             start=True, stop=False)
                        else:
                            pe.wait_ge(s["act_took"], due("act_took", it, Step("qh", z, st.stage, 0)))
                            pe.wait_ge(s["dve_took"], due("dve_took", it, Step("k", z, st.stage, half)))
                        nc.tensor.matmul(ps_score[u % 2][:].rearrange("p (h k) -> p h k", h=G),
                                         qh_t[z][:, half, b * SEQ:(b + 1) * SEQ],
                                         k_blk[z][:, place:place + G, b * SEQ:(b + 1) * SEQ],
                                         start=(st.stage >= 2), stop=True).then_inc(s["scored"], 1)
                    elif st.kind == "turn_p":
                        u = WHEN["turned_p", st] - 1
                        pe.wait_ge(s["scaled"], due("scaled", it, Step("scale", z, st.stage, st.part)))
                        for j in range(G):
                            last = nc.tensor.transpose(ps_turn[u % 2][:, j * P:(j + 1) * P], probs[:, u % 3, j, :],
                                                       ident[:])
                        last.then_inc(s["turned_p"], 1)
                    elif st.kind == "mix":
                        u = WHEN["mixed", st] - 1
                        b, half, _ = unit_of(st)
                        n, first, _ = OUT_OF[st]
                        if first and n < 2:
                            pe.wait_ge(out_taken, it * OUTS)
                        elif first:
                            pe.wait_ge(out_taken, it * OUTS + n - 1)
                        pe.wait_ge(s["act_took"], due("act_took", it, Step("v", z, 0 if st.stage < 2 else st.stage, 0)))
                        pe.wait_ge(s["pt_ready"], due("pt_ready", it, Step("turn_p", z, st.stage, st.part)))
                        for j in (0, 2, 1, 3) if st.stage < 2 else range(G):
                            if st.stage < 2:
                                head = 8 * half + G * (st.part % 2) + j
                                row = 32 * (head % 8 // 2)
                                v = v_pad[z][:, (A_HEADS // 2) * b + head // 2, 32 * (j % 2):32 * (j % 2) + 32]
                                start, stop = j % 2 == 0, j % 2 == 1
                            else:
                                row = 32 * j
                                v = v_row[z][:, b, half * P + row:half * P + row + 32]
                                start = stop = True
                            last = nc.tensor.matmul(ps_out[n % 2][row:row + 32, b * SEQ:(b + 1) * SEQ], v,
                                                    probs_t[:, u % 2, j, :], start=start, stop=stop)
                        last.then_inc(s["mixed"], 1)


def kernel(**inputs):
    import concourse.bacc as bacc
    from concourse.bass_utils import run_bass_kernel_spmd as run

    def arr(name):
        return np.asarray(inputs[name])

    def split_rows(w):
        w = w.reshape(w.shape[:-2] + (KT, P, w.shape[-1]))
        return np.ascontiguousarray(np.swapaxes(w, -3, -2))

    def cols(b):
        return np.ascontiguousarray(b.reshape(-1, KT, P).transpose(2, 0, 1))

    ctx = arr("ctx_1024").reshape(ITERS, CHAINS, TOK, D).transpose(0, 1, 3, 2)
    row = np.arange(P)
    own = np.concatenate([row[:, None] // A_DH == np.arange(8), row[:, None] // N_DH == np.arange(4)], 1)
    arrays = {
        "x": arr("x"),
        "ctx_t": split_rows(ctx),
        "w_cross": np.ascontiguousarray(
            split_rows(np.stack([arr(f"L0_xattn_W{n}").T for n in "qkvo"])).transpose(1, 0, 2, 3)),
        "b_cross": cols(np.stack([arr(f"L0_xattn_b{n}") for n in "qkv"])),
        "bo": arr("L0_xattn_bo"),
        "ln_g": arr("L0_ffn_ln_g"),
        "ln_b": arr("L0_ffn_ln_b"),
        "ew": arr("L0_ffn_ew").reshape(-1),
        "act_w": arr("L0_ffn_act_w"),
        "gates": np.concatenate([arr("g_xattn"), arr("g_ffn")]),
        "we": split_rows(arr("L0_ffn_We")),
        "we_t": split_rows(arr("L0_ffn_We").transpose(0, 2, 1)),
        "be_col": cols(arr("L0_ffn_be")),
        "wq": split_rows(arr("L0_ffn_Wq")),
        "wk": split_rows(arr("L0_ffn_Wk")),
        "wv": split_rows(arr("L0_ffn_Wv")),
        "wo": split_rows(arr("L0_ffn_Wo")),
        "ident": np.eye(P, dtype=np.float32),
        "band": np.where(abs(row[:, None] - row[None, :]) <= WINDOW // 2, 0.0, MASKED).astype(np.float32),
        "own": own.astype(np.float32),
    }
    nc = bacc.Bacc("TRN2", target_bir_lowering=False, num_devices=1)
    aps = {n: nc.dram_tensor(f"{n}_dram", v.shape, mybir.dt.from_np(v.dtype), kind="ExternalInput").ap()
           for n, v in arrays.items()}
    aps["out"] = nc.dram_tensor("out_dram", (BATCH, SEQ, D), F32, kind="ExternalOutput").ap()
    build(nc, aps)
    fed = {f"{n}_dram": v for n, v in arrays.items()}
    return run(nc, [fed], core_ids=[0]).results[0]["out_dram"]
```

```python
from collections import namedtuple
from contextlib import ExitStack

import numpy as np

import concourse.bass as bass
from concourse import mybir

P = 128
D = 256
SEQ = 128
BATCH = 32
PAIR = 2
TOK = PAIR * SEQ
CHAINS = 2
ITERS = BATCH // (PAIR * CHAINS)
KT = D // P
NODES = 6
MAX_PREV = 5
EDGES = 20
A_HEADS, A_DH = 16, 16
N_HEADS, N_DH = 8, 32
WINDOW = 128
G = 4
EPS_PRE = 1e-5
EPS_OUT = 1e-6
MASKED = -1e30

F32 = mybir.dt.float32
F32R = mybir.dt.float32r
ALU = mybir.AluOpType
ACT = mybir.ActivationFunctionType
AX_X = mybir.AxisListType.X

WQ, WQH, WK, WV, WO = range(5)
AQ, AK, AV, AO = range(4)

Step = namedtuple("Step", "kind z stage part")


def wiring():
    out, first = [], 0
    for c in range(NODES):
        n = min(c + 1, MAX_PREV)
        src = c - n
        out.append(dict(eq=first + n - 1, ek=first, ev=first + n // 2, q=c - 1, k=src, v=src + n // 2))
        first += n
    return out


WIRES = wiring()
CROSS = 0
STAGES = 1 + NODES
UNITS_OF = {s: 2 * N_HEADS // G for s in range(1, STAGES)} | {CROSS: 2 * A_HEADS // G}


def projections(z, s):
    def st(kind, part=0):
        return Step(kind, z, s, part)

    if s == CROSS:
        return [[st("moments")], [st("keys"), st("normalize")], [st("quad", 0), st("turn")], [st("v")], [st("q")],
                [st("quad", 1)]]
    if s == 1 and z == 0:
        return [[], [], [st("cross_out"), st("moments")], [st("normalize")], [st("turn")], [st("q")], [st("v")],
                [st("k", 0), st("k", 1), st("qh")]]
    if s == 1:
        return [[], [], [st("cross_out"), st("moments")], [st("normalize"), st("turn")], [st("q"), st("v")],
                [st("k", 0), st("k", 1), st("qh")]]
    if s == 2:
        return [[st("k", 0)], [st("k", 1)], [st("node_out")], [st("q")], [st("v")], [st("qh")]]
    if s < STAGES:
        return [[st("k", 0)], [st("v")], [st("node_out")], [st("q")], [st("k", 1)], [st("qh")]]
    return [[], [], [st("node_out")], [st("turn_back"), st("moments")], [], [st("normalize")]]


def attention(z, s):
    sc, nm, tr, pv = ([Step(k, z, s, u) for u in range(UNITS_OF[s])] for k in ("scores", "scale", "turn_p", "mix"))
    if s == CROSS:
        quad = [Step("quad", z, s, q) for q in range(4)]
        beat = [sc[0], -1, 0, sc[1], nm[0], -2, 1, sc[2], quad[2], nm[1], tr[0], -3, 2]
        for u in range(3, 8):
            beat += [sc[u], nm[u - 1], u, tr[u - 2], pv[u - 3]] + ([quad[3]] if u == 4 else [])
        return beat, {-1: [nm[7], tr[6], pv[5]], -2: [tr[7], pv[6]], -3: [pv[7]]}
    beat = [-1, sc[0], 0, -2, sc[1], -3, nm[0], 1, nm[1], sc[2], tr[0], 2, nm[2], pv[0], tr[1], sc[3], 3, tr[2],
            nm[3], 4, pv[1], 5]
    return beat, {-1: [tr[3], pv[2]], -2: [pv[3]]}


def beat_of(att, proj, tail):
    out = []
    for x in att:
        if isinstance(x, Step):
            out.append(x)
        elif x < 0:
            out += tail.get(x, [])
        elif x < len(proj):
            out += proj[x]
    return out


def plan():
    steps, tail = [], {}
    for s in range(STAGES):
        for z in range(CHAINS):
            att, new_tail = attention(z, s)
            proj = projections(1, s) if z == 0 else projections(0, s + 1)
            if z == 1 and s == STAGES - 1:
                ahead = projections(0, 0)
                proj = [p + (ahead[i] if i < len(ahead) else []) for i, p in enumerate(proj)]
            steps += beat_of(att, proj, tail)
            tail = new_tail
    return steps + tail[-1] + tail[-2] + [x for p in projections(1, STAGES) for x in p]


STEPS = plan()
AHEAD = [st for p in projections(0, 0) for st in p]

SIGNALS = {
    "projected": ("turn", "keys", "k", "v", "q", "qh", "node_out", "cross_out", "turn_back"),
    "act_took": ("turn", "keys", "v", "q", "qh"),
    "dve_took": ("k", "node_out", "cross_out"),
    "quad_ready": ("quad",),
    "var_ready": ("moments",),
    "rstd_ready": ("moments",),
    "normed": ("normalize",),
    "scored": ("scores",),
    "max_ready": ("scores",),
    "exp_done": ("scores",),
    "inv_ready": ("scale",),
    "scaled": ("scale",),
    "turned_p": ("turn_p",),
    "pt_ready": ("turn_p",),
    "mixed": ("mix",),
}
AHEAD_SIGNALS = ("projected", "act_took", "quad_ready", "var_ready", "rstd_ready", "normed")


def ordinals():
    when, total = {}, {}
    for ahead in (False, True):
        for name, kinds in SIGNALS.items():
            n = 0
            for st in STEPS:
                if st.kind in kinds and (st in AHEAD) == ahead:
                    n += 1
                    when[name, st] = n
            total[name, ahead] = n
    return when, total


WHEN, TOTAL = ordinals()
PROJ = [st for st in STEPS if st.kind in SIGNALS["projected"]]
UNITS = [st for st in STEPS if st.kind == "scores"]


def due(name, it, st, shift=0):
    total = TOTAL[name, st in AHEAD]
    return it * total + (shift * total + WHEN[name, st])


def bank_of(st):
    return PROJ.index(st) % 2


assert len(PROJ) % 2 == 0


def unit_of(st):
    if st.stage == CROSS:
        return st.part % 2, st.part // 4, G * (st.part // 2 % 2)
    return st.part % 2, st.part // 2, G * (st.part // 2)


def out_banks():
    out, n = {}, 0
    for st in STEPS:
        if st.kind == "mix":
            per = UNITS_OF[st.stage] // KT
            out[st] = (n, st.part % per == 0, st.part % per == per - 1)
            n += st.part % per == per - 1
    return out, n


OUT_OF, OUTS = out_banks()


def out_due(it, z, s, half):
    last = [OUT_OF[st] for st in OUT_OF if st.z == z and st.stage == s and OUT_OF[st][2]]
    return it * OUTS + (last[half][0] + 1)


def build(nc, a):
    ctx = ExitStack()
    with ctx:
        def sb(name, shape, dt=F32):
            return ctx.enter_context(nc.sbuf_tensor(name, shape, dt))

        def sem(name):
            return ctx.enter_context(nc.semaphore(name))

        w_cross = sb("w_cross", [P, 4, KT, D])
        w_node = sb("w_node", [P, NODES, 5, KT, D])
        b_cross = sb("b_cross", [P, 3, KT])
        b_node = sb("b_node", [P, NODES, 3, KT])
        be_col = sb("be_col", [P, EDGES, KT])
        rows = sb("rows", [P, 3, D])
        scalars = sb("scalars", [P, 3 * NODES + NODES + 2])
        gates = sb("gates", [P, 2])
        ident = sb("ident", [P, P])
        ident_r = sb("ident_r", [P, P], F32R)
        band_f = sb("band_f", [P, P])
        band_r = sb("band_r", [P, G, P], F32R)
        own = sb("own", [P, 8 + 4])
        idle = sb("idle", [P, 1])
        half_neg = sb("half_neg", [P, PAIR])
        stage_t = sb("stage_t", [P, 2, KT, D])
        stage_w = sb("stage_w", [P, 2, KT, D])

        def per_chain(name, shape, dt=F32):
            return [sb(f"{name}{z}", shape, dt) for z in range(CHAINS)]

        x_in = per_chain("x_in", [P, PAIR, D])
        x_bias = per_chain("x_bias", [P, PAIR, D])
        x1 = per_chain("x1", [P, PAIR, D])
        normed_x = per_chain("normed_x", [P, PAIR, D])
        result = per_chain("result", [P, PAIR, D])
        ctx_t = per_chain("ctx_t", [P, KT, TOK])
        stats = per_chain("stats", [P, PAIR, 6])
        moments = per_chain("moments", [P, PAIR, 2])
        var_eps = per_chain("var_eps", [P, PAIR])
        rstd = per_chain("rstd", [P, PAIR])
        SLOT = {-2: 3, -1: 0, 0: 1, 1: 2, 2: 3, 3: 4, 4: 0, 5: 2}
        node_t = per_chain("node_t", [P, 5, KT, TOK])
        q_t = per_chain("q_t", [P, KT, TOK])
        qh_t = per_chain("qh_t", [P, KT, TOK])
        k_t = per_chain("k_t", [P, KT, TOK])
        k_blk = per_chain("k_blk", [P, 2 * G, TOK])
        v_pad = per_chain("v_pad", [P, PAIR * A_HEADS // 2, 64])
        v_row = per_chain("v_row", [P, PAIR, D])
        o_t = per_chain("o_t", [P, KT, TOK])
        probs = sb("probs", [P, 3, G, SEQ])
        probs_t = sb("probs_t", [P, 2, G, SEQ])
        neg_max = sb("neg_max", [P, 4, G])
        row_sum = sb("row_sum", [P, 4, G])
        inv_sum = sb("inv_sum", [P, 4, G])

        def bank(name):
            return ctx.enter_context(nc.psum_tensor(name, [P, 512], F32))

        ps_proj = [bank(f"ps_proj{i}") for i in range(2)]
        ps_score = [bank(f"ps_score{i}") for i in range(2)]
        ps_turn = [bank(f"ps_turn{i}") for i in range(2)]
        ps_out = [bank(f"ps_out{i}") for i in range(2)]

        of_body = {name: sem(name) for name in SIGNALS}
        of_ahead = {name: sem(f"{name}_ahead") for name in AHEAD_SIGNALS}

        def sig(name, st):
            return of_ahead[name] if st in AHEAD else of_body[name]

        def at(name, it, st, shift=0):
            return sig(name, st), due(name, it, st, shift)

        out_taken = sem("out_taken")
        x_loaded = [sem(f"x_loaded{z}") for z in range(CHAINS)]
        ctx_loaded = [sem(f"ctx_loaded{z}") for z in range(CHAINS)]
        x_used = [sem(f"x_used{z}") for z in range(CHAINS)]
        x1_biased = sem("x1_biased")
        result_ready = sem("result_ready")
        pool_step = sem("pool_step")
        dve_step = {k: sem(f"dve_step{int(k)}") for k in (False, True)}
        stored = [sem(f"stored{z}") for z in range(CHAINS)]
        consts_in = sem("consts_in")
        weights_in = sem("weights_in")
        stage_in = [sem(f"stage_in{i}") for i in range(2)]
        gates_ready = sem("gates_ready")
        prep_act = sem("prep_act")
        prep_dve = sem("prep_dve")
        prep_pe = sem("prep_pe")
        zeroed = sem("zeroed")

        block = ctx.enter_context(nc.Block())

        x_v = a["x"].rearrange("(i z b) t d -> i z t b d", z=CHAINS, b=PAIR)
        ctx_v = a["ctx_t"]
        out_v = a["out"].rearrange("(i z b) t d -> i z t b d", z=CHAINS, b=PAIR)

        PRODUCTS = [(c, w, WIRES[c][e]) for c in range(NODES) for w, e in ((WK, "ek"), (WV, "ev"))]
        N_CONST = 7
        N_WEIGHT = 1 + 3 * NODES

        def ew(c, i):
            return scalars[:, 3 * c + i:3 * c + i + 1]

        def act_w(c):
            return scalars[:, 3 * NODES + c:3 * NODES + c + 1]

        def bcast(ap, n, m):
            return ap.rearrange("p (n o) -> p n o", o=1).to_broadcast([P, n, m])

        def on_all(dram, n):
            return dram.rearrange("(o n) -> o n", o=1).to_broadcast([P, n])

        @block.sync
        def _(sp):
            def load_x(it, z):
                sp.dma_start(x_in[z][:], x_v[it, z]).then_inc(x_loaded[z], 16)

            def load_ctx(it, z):
                sp.dma_start(ctx_t[z][:], ctx_v[it, z]).then_inc(ctx_loaded[z], 16)

            sp.dma_start(scalars[:, 0:3 * NODES], on_all(a["ew"], 3 * NODES)).then_inc(consts_in, 16)
            sp.dma_start(scalars[:, 3 * NODES:4 * NODES], on_all(a["act_w"], NODES)).then_inc(consts_in, 16)
            sp.dma_start(scalars[:, 4 * NODES:4 * NODES + 2], on_all(a["gates"], 2)).then_inc(consts_in, 16)
            for i, name in enumerate(("bo", "ln_g", "ln_b")):
                sp.dma_start(rows[:, i, :], on_all(a[name], D)).then_inc(consts_in, 16)
            sp.dma_start(b_cross[:], a["b_cross"]).then_inc(consts_in, 16)
            sp.dma_start(be_col[:], a["be_col"]).then_inc(consts_in, 16)
            sp.dma_start(ident[:], a["ident"]).then_inc(consts_in, 16)
            sp.dma_start(band_f[:], a["band"]).then_inc(consts_in, 16)
            sp.dma_start(own[:], a["own"]).then_inc(consts_in, 16)
            load_x(0, 0)
            load_x(0, 1)
            sp.dma_start(w_cross[:], a["w_cross"]).then_inc(weights_in, 16)
            load_ctx(0, 0)
            load_ctx(0, 1)
            for n, (c, w, e) in enumerate(PRODUCTS):
                if w == WK:
                    for place, src in ((WQ, a["we"][WIRES[c]["eq"]]), (WQH, a["wq"][c]), (WO, a["wo"][c])):
                        sp.dma_start(w_node[:, c, place], src).then_inc(weights_in, 16)
                if n >= 2:
                    sp.wait_ge(prep_pe, n - 1)
                sp.dma_start(stage_t[:, n % 2], a["we_t"][e]).then_inc(stage_in[n % 2], 16)
                sp.dma_start(stage_w[:, n % 2], a["wk" if w == WK else "wv"][c]).then_inc(stage_in[n % 2], 16)

            def store(it, z):
                sp.wait_ge(result_ready, it * CHAINS + z + 1)
                sp.dma_start(out_v[it, z], result[z][:]).then_inc(stored[z], 16)

            with sp.Fori(0, ITERS - 1) as it:
                for z in range(CHAINS):
                    sp.wait_ge(x_used[z], it + 1)
                    load_x(it + 1, z)
                for z in range(CHAINS):
                    sp.wait_ge(*at("projected", it, Step("v", z, CROSS, 0)))
                    load_ctx(it + 1, z)
                for z in range(CHAINS):
                    store(it, z)
            sp.wait_ge(x_used[0], ITERS)
            load_x(0, 0)
            sp.wait_ge(*at("projected", ITERS - 1, Step("v", 0, CROSS, 0)))
            load_ctx(0, 0)
            for z in range(CHAINS):
                store(ITERS - 1, z)
                sp.wait_ge(stored[z], 16 * ITERS)

        @block.gpsimd
        def _(pool):
            for z in range(CHAINS):
                nc.gpsimd.memset(v_pad[z][:], 0.0).then_inc(zeroed, 1)
            nc.gpsimd.memset(half_neg[:], -0.5).then_inc(zeroed, 1)
            pool.wait_ge(zeroed, 3)
            pool.wait_ge(prep_dve, 3)
            both = [P, PAIR, D]

            def step(it, st):
                z = st.z
                if st.kind == "moments":
                    pool.wait_ge(*at("var_ready", it, st))
                    nc.gpsimd.tensor_tensor(rstd[z][:], var_eps[z][:], half_neg[:],
                                            ALU.pow).then_inc(sig("rstd_ready", st), 1)
                elif st.kind == "normalize" and st.stage == CROSS:
                    pool.wait_ge(*at("normed", it, st))
                    nc.gpsimd.tensor_tensor(x_bias[z][:], x_in[z][:],
                                            rows[:, 0:1, :].to_broadcast(both), ALU.add).then_inc(x_used[z], 1)
                elif st.kind == "normalize" and st.stage == 1:
                    pool.wait_ge(*at("normed", it, st))
                    nc.gpsimd.tensor_tensor(x1[z][:], x1[z][:],
                                            rows[:, 2:3, :].to_broadcast(both), ALU.add).then_inc(x1_biased, 1)
                elif st.kind == "normalize":
                    pool.wait_ge(*at("normed", it, st))
                    nc.gpsimd.tensor_tensor(result[z][:], result[z][:],
                                            rows[:, 1:2, :].to_broadcast(both), ALU.mult).then_inc(pool_step, 1)
                    pool.wait_ge(pool_step, it * CHAINS + z + 1)
                    pool.wait_ge(x1_biased, it * CHAINS + CHAINS)
                    nc.gpsimd.tensor_tensor(result[z][:], result[z][:], x1[z][:],
                                            ALU.add).then_inc(result_ready, 1)
                elif st.kind == "scale":
                    u = WHEN["scaled", st] - 1
                    pool.wait_ge(*at("inv_ready", it, st))
                    p = probs[:, u % 3]
                    nc.gpsimd.tensor_tensor(p, p, bcast(inv_sum[:, u % 4, :], G, SEQ),
                                            ALU.mult).then_inc(sig("scaled", st), 1)

            for st in AHEAD:
                step(0, st)
            with pool.Fori(0, ITERS) as it:
                for st in STEPS:
                    step(it + 1 if st in AHEAD else it, st)

        @block.scalar
        def _(act):
            act.wait_ge(consts_in, 11 * 16)
            nc.scalar.activation(gates[:], scalars[:, 4 * NODES:4 * NODES + 2], ACT.Tanh).then_inc(gates_ready, 1)
            for n, (c, w, e) in enumerate(PRODUCTS):
                act.wait_ge(prep_pe, n + 1)
                i = 1 if w == WK else 2
                nc.scalar.activation(w_node[:, c, w].rearrange("p k d -> p (k d)"), ps_proj[n % 2][:], ACT.Copy,
                                     scale=ew(c, i)).then_inc(prep_act, 1)
                nc.scalar.activation(b_node[:, c, i], ps_score[n % 2][:, 0:KT], ACT.Copy,
                                     scale=ew(c, i)).then_inc(prep_act, 1)

            def take(it, st, bias, out):
                ps = ps_proj[bank_of(st)]
                for h in range(KT):
                    last = nc.scalar.activation(out[:, h, :], ps[:, h * TOK:(h + 1) * TOK], ACT.Identity,
                                                bias=bias[:, h:h + 1])
                last.then_inc(sig("act_took", st), 1)

            def step(it, st):
                z, c = st.z, st.stage - 1
                if st.kind in SIGNALS["act_took"]:
                    act.wait_ge(*at("projected", it, st))
                    ps = ps_proj[bank_of(st)]
                if st.kind == "turn":
                    slot = 3 if st.stage == CROSS else 0
                    nc.scalar.activation(node_t[z][:, slot].rearrange("p k t -> p (k t)"), ps[:],
                                         ACT.Copy).then_inc(sig("act_took", st), 1)
                elif st.kind == "keys":
                    take(it, st, b_cross[:, 1], k_t[z])
                elif st.kind == "q" and st.stage == CROSS:
                    take(it, st, b_cross[:, 0], qh_t[z])
                elif st.kind == "q":
                    take(it, st, b_node[:, c, 0], q_t[z])
                elif st.kind == "qh":
                    nc.scalar.activation(qh_t[z][:].rearrange("p k t -> p (k t)"), ps[:],
                                         ACT.Copy).then_inc(sig("act_took", st), 1)
                elif st.kind == "v" and st.stage == CROSS:
                    src = ps[:].rearrange("p (g e d) -> p g e d", e=2, d=A_DH)
                    nc.scalar.activation(v_pad[z][:, :, 0:A_DH], src[:, :, 0, :], ACT.Copy)
                    nc.scalar.activation(v_pad[z][:, :, 48:64], src[:, :, 1, :],
                                         ACT.Copy).then_inc(sig("act_took", st), 1)
                elif st.kind == "v":
                    nc.scalar.activation(v_row[z][:].rearrange("p b d -> p (b d)"), ps[:],
                                         ACT.Copy).then_inc(sig("act_took", st), 1)
                elif st.kind == "scores":
                    u = WHEN["scored", st] - 1
                    act.wait_ge(*at("max_ready", it, st))
                    for j in range(G):
                        last = nc.scalar.activation(
                            probs[:, u % 3, j, :], ps_score[u % 2][:, j * SEQ:(j + 1) * SEQ], ACT.Exp,
                            bias=neg_max[:, u % 4, j:j + 1], accum_out=row_sum[:, u % 4, j:j + 1])
                    last.then_inc(sig("exp_done", st), 1)
                elif st.kind == "mix" and OUT_OF[st][2]:
                    act.wait_ge(*at("mixed", it, st))
                    half = unit_of(st)[1]
                    bias = b_cross[:, 2] if st.stage == CROSS else b_node[:, c, 2]
                    nc.scalar.activation(o_t[z][:, half, :], ps_out[OUT_OF[st][0] % 2][:, 0:TOK], ACT.Identity,
                                         bias=bias[:, half:half + 1]).then_inc(out_taken, 1)

            for st in AHEAD:
                step(0, st)
            with act.Fori(0, ITERS) as it:
                for st in STEPS:
                    step(it + 1 if st in AHEAD else it, st)

        @block.vector
        def _(dve):
            dve.wait_ge(consts_in, 11 * 16)
            nc.vector.tensor_copy(ident_r[:], ident[:]).then_inc(prep_dve, 1)
            nc.vector.tensor_copy(band_r[:], band_f[:].rearrange("p (o k) -> p o k", o=1).to_broadcast([P, G, P]))\
                .then_inc(prep_dve, 1)
            dve.wait_ge(gates_ready, 1)
            nc.vector.tensor_scalar(rows[:, 0, :], rows[:, 0, :], gates[:, 0:1], None, ALU.mult)
            nc.vector.tensor_scalar(rows[:, 1:3, :], rows[:, 1:3, :], gates[:, 1:2], None, ALU.mult)\
                .then_inc(prep_dve, 1)
            nc.vector.tensor_scalar(b_cross[:, 0], b_cross[:, 0], A_DH ** -0.5, None, ALU.mult)
            for c in range(NODES):
                nc.vector.tensor_scalar(b_node[:, c, 0], be_col[:, WIRES[c]["eq"]], ew(c, 0), None, ALU.mult)
            dve.wait_ge(weights_in, 16 * N_WEIGHT)
            nc.vector.tensor_scalar(w_cross[:, AQ], w_cross[:, AQ], A_DH ** -0.5, None, ALU.mult)
            nc.vector.tensor_scalar(w_cross[:, AO], w_cross[:, AO], gates[:, 0:1], None, ALU.mult)
            for c in range(NODES):
                nc.vector.tensor_scalar(w_node[:, c, WQ], w_node[:, c, WQ], ew(c, 0), None, ALU.mult)
                nc.vector.tensor_scalar(w_node[:, c, WQH], w_node[:, c, WQH], N_DH ** -0.5, None, ALU.mult)
                last = nc.vector.tensor_scalar(w_node[:, c, WO], w_node[:, c, WO], act_w(c), None, ALU.mult)
            last.then_inc(prep_dve, 1)

            def rows_of(st):
                z = st.z
                if st.stage == CROSS:
                    return [x_in[z][:, b, :] for b in range(PAIR)], EPS_PRE
                if st.stage == 1:
                    return [x1[z][:, b, :] for b in range(PAIR)], EPS_PRE
                ps = ps_proj[bank_of(Step("turn_back", z, STAGES, 0))]
                return [ps[:, b * D:(b + 1) * D] for b in range(PAIR)], EPS_OUT

            def step(it, st):
                z, c = st.z, st.stage - 1
                if st.kind in ("k", "node_out", "cross_out"):
                    dve.wait_ge(*at("projected", it, st))
                    ps = ps_proj[bank_of(st)]
                if st.kind == "moments":
                    if st.stage == CROSS:
                        dve.wait_ge(x_loaded[z], it * 16 + 16)
                    elif st.stage == 1:
                        dve.wait_ge(*at("dve_took", it, Step("cross_out", z, 1, 0)))
                    else:
                        dve.wait_ge(*at("projected", it, Step("turn_back", z, STAGES, 0)))
                    rows_in, eps = rows_of(st)
                    own_order = dve_step[st in AHEAD]
                    n = 2 * (due("var_ready", it, st) - 1)
                    for b in range(PAIR):
                        last = nc.vector.bn_stats(stats[z][:, b, :], rows_in[b])
                    last.then_inc(own_order, 1)
                    dve.wait_ge(own_order, n + 1)
                    nc.vector.memset(idle[:], 0.0)
                    for b in range(PAIR):
                        last = nc.vector.bn_aggr(moments[z][:, b, :], stats[z][:, b, :])
                    last.then_inc(own_order, 1)
                    dve.wait_ge(own_order, n + 2)
                    nc.vector.tensor_scalar(var_eps[z][:], moments[z][:, :, 1], eps, None,
                                            ALU.add).then_inc(sig("var_ready", st), 1)
                elif st.kind == "normalize":
                    rows_in, _ = rows_of(st)
                    out = result[z] if st.stage == STAGES else normed_x[z]
                    if st.stage == STAGES:
                        dve.wait_ge(stored[z], it * 16)
                    dve.wait_ge(*at("rstd_ready", it, Step("moments", z, st.stage, 0)))
                    for b in range(PAIR):
                        last = nc.vector.tensor_scalar(out[:, b, :], rows_in[b], moments[z][:, b, 0:1],
                                                       rstd[z][:, b:b + 1], ALU.subtract, ALU.mult)
                    last.then_inc(sig("normed", st), 1)
                elif st.kind == "cross_out":
                    dve.wait_ge(x_used[z], it + 1)
                    dve.wait_ge(result_ready, it * CHAINS)
                    nc.vector.tensor_tensor(x1[z][:].rearrange("p b d -> p (b d)"), ps[:],
                                            x_bias[z][:].rearrange("p b d -> p (b d)"),
                                            ALU.add).then_inc(sig("dve_took", st), 1)
                elif st.kind == "k":
                    half = st.part
                    keys = ps[:, 0:TOK].rearrange("p (o t) -> p o t", o=1).to_broadcast([P, G, TOK])
                    nc.vector.scalar_tensor_tensor(
                        out=k_blk[z][:, G * half:G * half + G, :], in0=keys, scalar=b_node[:, c, 1, half:half + 1],
                        in1=bcast(own[:, 8:12], G, TOK), op0=ALU.add, op1=ALU.mult).then_inc(sig("dve_took", st), 1)
                elif st.kind == "quad":
                    half, place = st.part // 2, G * (st.part % 2)
                    dve.wait_ge(*at("act_took", it, Step("keys", z, CROSS, 0)))
                    if st.part >= 2:
                        dve.wait_ge(*at("scored", it, Step("scores", z, CROSS, 2 * (st.part - 2) + 1)))
                    nc.vector.tensor_tensor(
                        k_blk[z][:, place:place + G, :], k_t[z][:, half:half + 1, :].to_broadcast([P, G, TOK]),
                        bcast(own[:, place:place + G], G, TOK), ALU.mult).then_inc(sig("quad_ready", st), 1)
                elif st.kind == "node_out":
                    nc.vector.tensor_tensor(node_t[z][:, SLOT[c - 1]].rearrange("p k t -> p (k t)"), ps[:],
                                            q_t[z][:].rearrange("p k t -> p (k t)"),
                                            ALU.add).then_inc(sig("dve_took", st), 1)
                elif st.kind == "scores":
                    u = WHEN["scored", st] - 1
                    dve.wait_ge(*at("scored", it, st))
                    nc.vector.tensor_reduce(neg_max[:, u % 4, :],
                                            ps_score[u % 2][:].rearrange("p (h k) -> p h k", h=G),
                                            AX_X, ALU.max, negate=True).then_inc(sig("max_ready", st), 1)
                elif st.kind == "scale":
                    u = WHEN["scaled", st] - 1
                    dve.wait_ge(*at("exp_done", it, Step("scores", z, st.stage, st.part)))
                    nc.vector.reciprocal(inv_sum[:, u % 4, :], row_sum[:, u % 4, :]).then_inc(sig("inv_ready", st), 1)
                elif st.kind == "turn_p":
                    u = WHEN["turned_p", st] - 1
                    dve.wait_ge(*at("turned_p", it, st))
                    nc.vector.tensor_copy(probs_t[:, u % 2].rearrange("p h q -> p (h q)"),
                                          ps_turn[u % 2][:]).then_inc(sig("pt_ready", st), 1)

            for st in AHEAD:
                step(0, st)
            with dve.Fori(0, ITERS) as it:
                for st in STEPS:
                    step(it + 1 if st in AHEAD else it, st)

        @block.tensor
        def _(pe):
            def project(ps, col, w, src, half):
                for k in range(KT):
                    last = nc.tensor.matmul(ps[:, col:col + TOK], w[:, k, half * P:(half + 1) * P], src[:, k, :],
                                            start=(k == 0), stop=(k == KT - 1))
                return last

            def project_rows(ps, w, src):
                for b in range(PAIR):
                    for k in range(KT):
                        last = nc.tensor.matmul(ps[:, b * D:(b + 1) * D], src[:, k, b * SEQ:(b + 1) * SEQ], w[:, k, :],
                                                start=(k == 0), stop=(k == KT - 1))
                return last

            pe.wait_ge(consts_in, 11 * 16)
            for n, (c, w, e) in enumerate(PRODUCTS):
                pe.wait_ge(stage_in[n % 2], 32 * (n // 2 + 1))
                if n >= 2:
                    pe.wait_ge(prep_act, 2 * (n - 1))
                lhs, rhs = stage_t[:, n % 2], stage_w[:, n % 2]
                for h in range(KT):
                    for k in range(KT):
                        nc.tensor.matmul(ps_score[n % 2][:, h:h + 1], rhs[:, k, h * P:(h + 1) * P],
                                         be_col[:, e, k:k + 1], start=(k == 0), stop=(k == KT - 1))
                for h in range(KT):
                    for k in range(KT):
                        last = nc.tensor.matmul(ps_proj[n % 2][:, h * D:(h + 1) * D], lhs[:, k, h * P:(h + 1) * P],
                                                rhs[:, k, :], start=(k == 0), stop=(k == KT - 1))
                last.then_inc(prep_pe, 1)
            pe.wait_ge(prep_act, 2 * len(PRODUCTS))
            pe.wait_ge(prep_dve, 4)
            pe.wait_ge(zeroed, 3)

            def bank_for(it, st):
                before = PROJ[PROJ.index(st) - 2]
                shift = (before in AHEAD) - (st in AHEAD) - (PROJ.index(st) < 2)
                if before.kind == "turn_back":
                    pe.wait_ge(*at("normed", it, Step("normalize", before.z, STAGES, 0), shift))
                elif before.kind in SIGNALS["act_took"]:
                    pe.wait_ge(*at("act_took", it, before, shift))
                else:
                    pe.wait_ge(*at("dve_took", it, before, shift))
                return ps_proj[bank_of(st)]

            def bank_in_turn(n):
                st, before = ahead_proj[n], ahead_proj[n - 1]
                if n:
                    pe.wait_ge(*at("act_took", 0, before))
                return ps_proj[bank_of(st)]

            ahead_proj = [st for st in AHEAD if st.kind in SIGNALS["projected"]]

            def node_ready(it, z, n):
                if n == -1:
                    pe.wait_ge(*at("act_took", it, Step("turn", z, 1, 0)))
                else:
                    pe.wait_ge(*at("dve_took", it, Step("node_out", z, n + 2, 0)))
                return node_t[z][:, SLOT[n]]

            def step(it, st, before_loop=False):
                z, c = st.z, st.stage - 1
                if st.kind in SIGNALS["projected"]:
                    ps = bank_in_turn(ahead_proj.index(st)) if before_loop else bank_for(it, st)
                if st.kind == "turn":
                    pe.wait_ge(*at("normed", it, Step("normalize", z, st.stage, 0)))
                    for k in range(KT):
                        for b in range(PAIR):
                            last = nc.tensor.transpose(ps[:, (k * PAIR + b) * P:(k * PAIR + b + 1) * P],
                                                       normed_x[z][:, b, k * P:(k + 1) * P], ident[:])
                    last.then_inc(sig("projected", st), 1)
                elif st.kind == "turn_back":
                    last_node = node_ready(it, z, NODES - 1)
                    for b in range(PAIR):
                        for k in range(KT):
                            last = nc.tensor.transpose(ps[:, (b * KT + k) * P:(b * KT + k + 1) * P],
                                                       last_node[:, k, b * SEQ:(b + 1) * SEQ], ident[:])
                    last.then_inc(sig("projected", st), 1)
                elif st.kind == "keys":
                    pe.wait_ge(ctx_loaded[z], it * 16 + 16)
                    project(ps, 0, w_cross[:, AK], ctx_t[z], 0)
                    project(ps, TOK, w_cross[:, AK], ctx_t[z], 1).then_inc(sig("projected", st), 1)
                elif st.kind == "k":
                    project(ps, 0, w_node[:, c, WK], node_ready(it, z, WIRES[c]["k"]), st.part)\
                        .then_inc(sig("projected", st), 1)
                elif st.kind == "v" and st.stage == CROSS:
                    pe.wait_ge(ctx_loaded[z], it * 16 + 16)
                    project_rows(ps, w_cross[:, AV], ctx_t[z]).then_inc(sig("projected", st), 1)
                elif st.kind == "v":
                    project_rows(ps, w_node[:, c, WV], node_ready(it, z, WIRES[c]["v"]))\
                        .then_inc(sig("projected", st), 1)
                elif st.kind == "q":
                    if st.stage == CROSS:
                        pe.wait_ge(*at("act_took", it, Step("turn", z, 0, 0)))
                        w, src = w_cross[:, AQ], node_t[z][:, 3]
                    else:
                        w, src = w_node[:, c, WQ], node_ready(it, z, WIRES[c]["q"])
                    project(ps, 0, w, src, 0)
                    project(ps, TOK, w, src, 1).then_inc(sig("projected", st), 1)
                elif st.kind == "qh":
                    pe.wait_ge(*at("act_took", it, Step("q", z, st.stage, 0)))
                    project(ps, 0, w_node[:, c, WQH], q_t[z], 0)
                    project(ps, TOK, w_node[:, c, WQH], q_t[z], 1).then_inc(sig("projected", st), 1)
                elif st.kind == "cross_out":
                    pe.wait_ge(out_taken, out_due(it, z, CROSS, 1))
                    project_rows(ps, w_cross[:, AO], o_t[z]).then_inc(sig("projected", st), 1)
                elif st.kind == "node_out":
                    pe.wait_ge(out_taken, out_due(it, z, st.stage - 1, 1))
                    project(ps, 0, w_node[:, c - 1, WO], o_t[z], 0)
                    project(ps, TOK, w_node[:, c - 1, WO], o_t[z], 1).then_inc(sig("projected", st), 1)
                elif st.kind == "scores":
                    u = WHEN["scored", st] - 1
                    b, half, place = unit_of(st)
                    if u < 2:
                        pe.wait_ge(of_body["exp_done"], it * TOTAL["exp_done", False])
                    else:
                        pe.wait_ge(*at("exp_done", it, UNITS[u - 2]))
                    if st.stage == CROSS:
                        pe.wait_ge(*at("act_took", it, Step("q", z, CROSS, 0)))
                        pe.wait_ge(*at("quad_ready", it, Step("quad", z, CROSS, st.part // 2)))
                        nc.tensor.matmul(ps_score[u % 2][:], ident_r[:], band_r[:].rearrange("p h k -> p (h k)"),
                                         start=True, stop=False)
                    else:
                        pe.wait_ge(*at("act_took", it, Step("qh", z, st.stage, 0)))
                        pe.wait_ge(*at("dve_took", it, Step("k", z, st.stage, half)))
                    nc.tensor.matmul(ps_score[u % 2][:].rearrange("p (h k) -> p h k", h=G),
                                     qh_t[z][:, half, b * SEQ:(b + 1) * SEQ],
                                     k_blk[z][:, place:place + G, b * SEQ:(b + 1) * SEQ],
                                     start=(st.stage != CROSS), stop=True).then_inc(sig("scored", st), 1)
                elif st.kind == "turn_p":
                    u = WHEN["turned_p", st] - 1
                    pe.wait_ge(*at("scaled", it, Step("scale", z, st.stage, st.part)))
                    for j in range(G):
                        last = nc.tensor.transpose(ps_turn[u % 2][:, j * P:(j + 1) * P], probs[:, u % 3, j, :],
                                                   ident[:])
                    last.then_inc(sig("turned_p", st), 1)
                elif st.kind == "mix":
                    u = WHEN["mixed", st] - 1
                    b, half, _ = unit_of(st)
                    n, first, _ = OUT_OF[st]
                    if first and n < 2:
                        pe.wait_ge(out_taken, it * OUTS)
                    elif first:
                        pe.wait_ge(out_taken, it * OUTS + n - 1)
                    pe.wait_ge(*at("act_took", it, Step("v", z, st.stage, 0)))
                    pe.wait_ge(*at("pt_ready", it, Step("turn_p", z, st.stage, st.part)))
                    for j in (0, 2, 1, 3) if st.stage == CROSS else range(G):
                        if st.stage == CROSS:
                            head = G * (st.part // 2) + j
                            row = 32 * (head % 8 // 2)
                            v = v_pad[z][:, (A_HEADS // 2) * b + head // 2, 32 * (j % 2):32 * (j % 2) + 32]
                            start, stop = j % 2 == 0, j % 2 == 1
                        else:
                            row = 32 * j
                            v = v_row[z][:, b, half * P + row:half * P + row + 32]
                            start = stop = True
                        last = nc.tensor.matmul(ps_out[n % 2][row:row + 32, b * SEQ:(b + 1) * SEQ], v,
                                                probs_t[:, u % 2, j, :], start=start, stop=stop)
                    last.then_inc(sig("mixed", st), 1)

            for st in AHEAD:
                step(0, st, True)
            with pe.Fori(0, ITERS) as it:
                for st in STEPS:
                    step(it + 1 if st in AHEAD else it, st)


def kernel(**inputs):
    import concourse.bacc as bacc
    from concourse.bass_utils import run_bass_kernel_spmd as run

    def arr(name):
        return np.asarray(inputs[name])

    def split_rows(w):
        w = w.reshape(w.shape[:-2] + (KT, P, w.shape[-1]))
        return np.ascontiguousarray(np.swapaxes(w, -3, -2))

    def cols(b):
        return np.ascontiguousarray(b.reshape(-1, KT, P).transpose(2, 0, 1))

    ctx = arr("ctx_1024").reshape(ITERS, CHAINS, TOK, D).transpose(0, 1, 3, 2)
    row = np.arange(P)
    own = np.concatenate([row[:, None] // A_DH == np.arange(8), row[:, None] // N_DH == np.arange(4)], 1)
    arrays = {
        "x": arr("x"),
        "ctx_t": split_rows(ctx),
        "w_cross": np.ascontiguousarray(
            split_rows(np.stack([arr(f"L0_xattn_W{n}").T for n in "qkvo"])).transpose(1, 0, 2, 3)),
        "b_cross": cols(np.stack([arr(f"L0_xattn_b{n}") for n in "qkv"])),
        "bo": arr("L0_xattn_bo"),
        "ln_g": arr("L0_ffn_ln_g"),
        "ln_b": arr("L0_ffn_ln_b"),
        "ew": arr("L0_ffn_ew").reshape(-1),
        "act_w": arr("L0_ffn_act_w"),
        "gates": np.concatenate([arr("g_xattn"), arr("g_ffn")]),
        "we": split_rows(arr("L0_ffn_We")),
        "we_t": split_rows(arr("L0_ffn_We").transpose(0, 2, 1)),
        "be_col": cols(arr("L0_ffn_be")),
        "wq": split_rows(arr("L0_ffn_Wq")),
        "wk": split_rows(arr("L0_ffn_Wk")),
        "wv": split_rows(arr("L0_ffn_Wv")),
        "wo": split_rows(arr("L0_ffn_Wo")),
        "ident": np.eye(P, dtype=np.float32),
        "band": np.where(abs(row[:, None] - row[None, :]) <= WINDOW // 2, 0.0, MASKED).astype(np.float32),
        "own": own.astype(np.float32),
    }
    nc = bacc.Bacc("TRN2", target_bir_lowering=False, num_devices=1)
    aps = {n: nc.dram_tensor(f"{n}_dram", v.shape, mybir.dt.from_np(v.dtype), kind="ExternalInput").ap()
           for n, v in arrays.items()}
    aps["out"] = nc.dram_tensor("out_dram", (BATCH, SEQ, D), F32, kind="ExternalOutput").ap()
    build(nc, aps)
    fed = {f"{n}_dram": v for n, v in arrays.items()}
    return run(nc, [fed], core_ids=[0]).results[0]["out_dram"]
```

```python
from collections import namedtuple
from contextlib import ExitStack

import numpy as np

import concourse.bass as bass
from concourse import mybir

P = 128
D = 256
SEQ = 128
BATCH = 32
PAIR = 2
TOK = PAIR * SEQ
CHAINS = 2
ITERS = BATCH // (PAIR * CHAINS)
KT = D // P
NODES = 6
MAX_PREV = 5
EDGES = 20
A_HEADS, A_DH = 16, 16
N_HEADS, N_DH = 8, 32
WINDOW = 128
G = 4
EPS_PRE = 1e-5
EPS_OUT = 1e-6
MASKED = -1e30

F32 = mybir.dt.float32
F32R = mybir.dt.float32r
ALU = mybir.AluOpType
ACT = mybir.ActivationFunctionType
AX_X = mybir.AxisListType.X

WQH, WK, WV, WQ, WO = range(5)
IN, OUT = 3, 2
HIGH, REST = 0, 1
AQ, AK, AV, AO = range(4)

Step = namedtuple("Step", "kind z stage part")


def wiring():
    out, first = [], 0
    for c in range(NODES):
        n = min(c + 1, MAX_PREV)
        src = c - n
        out.append(dict(eq=first + n - 1, ek=first, ev=first + n // 2, q=c - 1, k=src, v=src + n // 2))
        first += n
    return out


WIRES = wiring()
CROSS = 0
STAGES = 1 + NODES
UNITS_OF = {s: 2 * N_HEADS // G for s in range(1, STAGES)} | {CROSS: 2 * A_HEADS // G}


NAMES = {"S": "scores", "D": "scale", "T": "turn_p", "M": "mix", "R": "out_rest", "Q": "quad"}
BEATS = {
    "cross_cross": """split Q2 S0 S1 moments D0 S2 D1 Q3 quad1 normalize S3 keys D2 T0 S4 turn T1 T2 D3 M0 quad0 D4 v S5
        M1 q D5 S6 T3 S7 T4 D6 T5 M2 M3""",
    "cross_first": """D7' S0 R0' Q2 T6' M4' S1 M5' T7' D0 S2 M6' M7' R1' S3 D1 D2 T0 cross_out T1 D3 moments S4 M0
        normalize T2 T3 Q3 M1 turn D4 M2 S5 k1 qh D5 T4 S6 M3 S7 D6 k0 T5 v""",
    "first_first": """M4' D7' T6' R0' M5' S0 T7' R1' M6' S1 M7' D0 S2 cross_out D1 T0 normalize moments T1 D2 turn M0 S3
        M1 k0 qh T2 k1 D3 R0 v""",
    "node_second": "S0 T3' M2' S1 D0 k1 M3' R1' S2 k0 D1 T0 node_out T1 D2 S3 M0 T2 qh R0 D3 v M1",
    "node_node": "S0 T3' k0 M2' v S1 D0 M3' R1' S2 node_out T0 D1 S3 k1 T1 D2 qh M0 T2 D3 R0 M1",
    "node_last": """S0 ahead_split T3' M2' S1 D0 M3' R1' S2 D1 ahead_moments last_out T0 S3 turn_back D2 moments M0 T1
        T2 ahead_normalize D3 ahead_keys M1 R0 ahead_quad0 normalize ahead_quad1""",
    "end": "R1' T3' ahead_turn M2' M3' last_out ahead_q moments turn_back normalize ahead_v",
}
BEAT_OF = {(CROSS, 0): "cross_cross", (CROSS, 1): "cross_first", (1, 0): "first_first", (1, 1): "node_second",
           (2, 0): "node_second", (STAGES - 1, 1): "node_last"}


def spell(token, s, z):
    if token.startswith("ahead_"):
        own, s, z, token = False, CROSS, 0, token[len("ahead_"):]
    elif token[0] in NAMES:
        own = True
        if token.endswith("'"):
            s, z, token = (s, 0, token[:-1]) if z else (s - 1, 1, token[:-1])
    else:
        own, s, z = False, s + z, 1 - z
    kind, part = (token[:-1], int(token[-1])) if token[-1].isdigit() else (token, 0)
    return Step(NAMES[kind] if own else kind, z, s, part)


def plan():
    steps = []
    for s in range(STAGES):
        for z in range(CHAINS):
            steps += [spell(t, s, z) for t in BEATS[BEAT_OF.get((s, z), "node_node")].split()]
    return steps + [spell(t, STAGES, 0) for t in BEATS["end"].split()]


STEPS = plan()
AHEAD = [spell(t, 0, 0) for t in " ".join(BEATS.values()).split() if t.startswith("ahead_")]
assert len(set(STEPS)) == len(STEPS) and set(AHEAD) < set(STEPS)

TENSOR_TIME = {"scores": 9, "turn_p": 4, "mix": 3, "k": 7, "v": 13, "q": 13, "qh": 13, "keys": 13, "node_out": 27,
               "last_out": 27, "cross_out": 13, "turn": 4, "turn_back": 4}
LAG = {
        "pe": {},
        "dve": {"moments": -7, "scale": -7, "quad": 22, "normalize": -5, "node_out": 30, "turn_p": -2,
            "split": -7, "k": 5, "scores": 2, "out_rest": -1, "turn": 6},
        "act": {"mix": -10, "node_out": 20, "turn": -7, "keys": -7, "scores": 3, "v": 15, "qh": -7, "q": 6},
        "pool": {"normalize": 29, "scale": 13, "moments": 17, "split": 29},
}


def order_of(engine):
    reached, at_step = 0, {}
    for st in STEPS:
        at_step[st] = reached + LAG[engine].get(st.kind, 0)
        reached += TENSOR_TIME.get(st.kind, 0)
    return sorted(STEPS, key=at_step.get)


ORDER = {engine: order_of(engine) for engine in LAG}
FIRST = {engine: [st for st in ORDER[engine] if st in AHEAD] for engine in ORDER}

SIGNALS = {
    "projected": ("turn", "keys", "k", "v", "q", "qh", "node_out", "cross_out", "last_out", "turn_back"),
    "act_took": ("turn", "keys", "v", "q", "qh", "node_out", "last_out"),
    "dve_took": ("turn", "k", "node_out", "cross_out"),
    "ctx_high": ("split",),
    "ctx_split": ("split",),
    "quad_ready": ("quad",),
    "var_ready": ("moments",),
    "rstd_ready": ("moments",),
    "normed": ("normalize",),
    "scored": ("scores",),
    "max_ready": ("scores",),
    "exp_done": ("scores",),
    "inv_ready": ("scale",),
    "scaled": ("scale",),
    "turned_p": ("turn_p",),
    "pt_ready": ("turn_p",),
    "mixed": ("mix",),
}
MAKER = {"projected": "pe", "act_took": "act", "dve_took": "dve", "ctx_high": "dve", "ctx_split": "pool",
         "quad_ready": "dve", "var_ready": "dve", "rstd_ready": "pool", "normed": "dve", "scored": "pe",
         "max_ready": "dve", "exp_done": "act", "inv_ready": "dve", "scaled": "pool", "turned_p": "pe",
         "pt_ready": "dve", "mixed": "pe"}
AHEAD_SIGNALS = ("projected", "act_took", "dve_took", "ctx_high", "ctx_split", "quad_ready", "var_ready",
                 "rstd_ready", "normed")


def ordinals():
    when, total = {}, {}
    for ahead in (False, True):
        for name, kinds in SIGNALS.items():
            n = 0
            for st in ORDER[MAKER[name]]:
                if st.kind in kinds and (st in AHEAD) == ahead:
                    n += 1
                    when[name, st] = n
            total[name, ahead] = n
    return when, total


WHEN, TOTAL = ordinals()
PROJ = [st for st in STEPS if st.kind in SIGNALS["projected"]]
UNITS = [(st.z, st.stage, st.part) for st in STEPS if st.kind == "scores"]


def number(st):
    return UNITS.index((st.z, st.stage, st.part))


def of_unit(kind, u):
    return Step(kind, *UNITS[u])


def due(name, it, st, shift=0):
    total = TOTAL[name, st in AHEAD]
    return it * total + (shift * total + WHEN[name, st])


LAST_WITH = {s: (UNITS_OF[s] - 1 - (2 if s == CROSS else UNITS_OF[s] // 2), UNITS_OF[s] - 1) for s in UNITS_OF}


def bank_of(st):
    return PROJ.index(st) % 2


assert len(PROJ) % 2 == 0


def unit_of(st):
    if st.stage == CROSS:
        return st.part % 2, st.part // 4, G * (st.part // 2 % 2)
    return st.part % 2, st.part // 2, G * (st.part // 2)


def out_banks():
    out, n = {}, 0
    for st in STEPS:
        if st.kind == "mix":
            per = UNITS_OF[st.stage] // KT
            out[st] = (n, st.part % per == 0, st.part % per == per - 1)
            n += st.part % per == per - 1
    return out, n


OUT_OF, OUTS = out_banks()


def out_due(it, z, s, half):
    last = [OUT_OF[st] for st in OUT_OF if st.z == z and st.stage == s and OUT_OF[st][2]]
    return it * OUTS + (last[half][0] + 1)


def build(nc, a):
    ctx = ExitStack()
    with ctx:
        STAGED = 4

        def sb(name, shape, dt=F32):
            return ctx.enter_context(nc.sbuf_tensor(name, shape, dt))

        def sem(name):
            return ctx.enter_context(nc.semaphore(name))

        w_cross = sb("w_cross", [P, 4, 2, KT, D], F32R)
        w_in = [sb(f"w_in{i}", [P, IN, 2, KT, D], F32R) for i in range(2)]
        w_out = [sb(f"w_out{i}", [P, OUT, 2, KT, D], F32R) for i in range(2)]
        b_cross = sb("b_cross", [P, 3, KT])
        b_node = sb("b_node", [P, NODES, 4, KT])
        be_col = sb("be_col", [P, EDGES, KT])
        rows = sb("rows", [P, 3, D])
        scalars = sb("scalars", [P, 3 * NODES + NODES + 2])
        gates = sb("gates", [P, 2])
        ident = sb("ident", [P, P])
        ident_r = sb("ident_r", [P, P], F32R)
        band_f = sb("band_f", [P, P])
        band_r = sb("band_r", [P, G, P], F32R)
        own = sb("own", [P, 8 + 4])
        idle = sb("idle", [P, 1])
        half_neg = sb("half_neg", [P, PAIR])
        scales = sb("scales", [P, 4 + 5 * NODES])

        def per_chain(name, shape, dt=F32):
            return [sb(f"{name}{z}", shape, dt) for z in range(CHAINS)]

        x_in = per_chain("x_in", [P, PAIR, D])
        x_bias = per_chain("x_bias", [P, PAIR, D])
        x1 = per_chain("x1", [P, PAIR, D])
        normed_x = per_chain("normed_x", [P, PAIR, D])
        result = per_chain("result", [P, PAIR, D])
        ctx_t = per_chain("ctx_t", [P, KT, TOK])
        ctx_s = per_chain("ctx_s", [P, 2, KT, TOK], F32R)
        stats = sb("stats", [P, CHAINS + 1, PAIR, 6])
        moments = sb("moments", [P, CHAINS + 1, PAIR, 2])
        var_eps = sb("var_eps", [P, CHAINS + 1, PAIR])
        rstd = sb("rstd", [P, CHAINS + 1, PAIR])
        SLOT = {-2: 3, -1: 0, 0: 1, 1: 2, 2: 3, 3: 4, 4: 0}
        node_t = per_chain("node_t", [P, 5, 2, KT, TOK], F32R)
        qh_t = per_chain("qh_t", [P, KT, TOK])
        k_t = per_chain("k_t", [P, KT, TOK])
        k_blk = per_chain("k_blk", [P, 2 * G, TOK])
        v_pad = per_chain("v_pad", [P, PAIR * A_HEADS // 2, 64])
        v_row = per_chain("v_row", [P, PAIR, D])
        o_t = per_chain("o_t", [P, 2, KT, TOK], F32R)
        probs = sb("probs", [P, 3, G, SEQ])
        probs_t = sb("probs_t", [P, 2, G, SEQ])
        neg_max = sb("neg_max", [P, 4, G])
        row_sum = sb("row_sum", [P, 4, G])
        inv_sum = sb("inv_sum", [P, 4, G])

        def bank(name):
            return ctx.enter_context(nc.psum_tensor(name, [P, 512], F32))

        ps_proj = [bank(f"ps_proj{i}") for i in range(2)]
        ps_score = [bank(f"ps_score{i}") for i in range(2)]
        ps_turn = [bank(f"ps_turn{i}") for i in range(2)]
        ps_out = [bank(f"ps_out{i}") for i in range(2)]

        of_body = {name: sem(name) for name in SIGNALS}
        of_ahead = {name: sem(f"{name}_ahead") for name in AHEAD_SIGNALS}

        def sig(name, st):
            return of_ahead[name] if st in AHEAD else of_body[name]

        def at(name, it, st, shift=0):
            return sig(name, st), due(name, it, st, shift)

        out_high = sem("out_high")
        out_taken = sem("out_taken")
        x_loaded = [sem(f"x_loaded{z}") for z in range(CHAINS)]
        ctx_loaded = [sem(f"ctx_loaded{z}") for z in range(CHAINS)]
        x_used = [sem(f"x_used{z}") for z in range(CHAINS)]
        x1_biased = sem("x1_biased")
        result_ready = sem("result_ready")
        pool_step = sem("pool_step")
        dve_step = {k: sem(f"dve_step{int(k)}") for k in (False, True)}
        stored = [sem(f"stored{z}") for z in range(CHAINS)]
        consts_in = sem("consts_in")
        scalars_in = sem("scalars_in")
        biases_in = sem("biases_in")
        stage_in = [sem(f"stage_in{i}") for i in range(STAGED)]
        w_stored = [sem(f"w_stored{i}") for i in range(IN + OUT)]
        in_loaded = [sem(f"in_loaded{i}") for i in range(2)]
        out_loaded = [sem(f"out_loaded{i}") for i in range(2)]
        gates_ready = sem("gates_ready")
        scales_ready = sem("scales_ready")
        prep_pe = sem("prep_pe")
        prep_high = sem("prep_high")
        prep_rest = sem("prep_rest")
        prep_dve = sem("prep_dve")
        zeroed = sem("zeroed")

        block = ctx.enter_context(nc.Block())

        x_v = a["x"].rearrange("(i z b) t d -> i z t b d", z=CHAINS, b=PAIR)
        ctx_v = a["ctx_t"]
        out_v = a["out"].rearrange("(i z b) t d -> i z t b d", z=CHAINS, b=PAIR)

        ITEMS = []
        for c in range(NODES):
            wire = WIRES[c]
            ITEMS += [(c, WQH, wire["eq"], a["wq"][c]), (c, WK, wire["ek"], a["wk"][c]), (c, WV, wire["ev"], a["wv"][c]),
                      (c, WQ, None, a["we"][wire["eq"]]), (c, WO, None, a["wo"][c])]
        ITEMS[-IN - OUT:-IN - OUT] = [(None, w, None, a["w_cross"][w]) for w in range(4)]
        PRODUCTS = [n for n, item in enumerate(ITEMS) if item[2] is not None]
        CROSS_SCALES = NODES * (IN + OUT)

        def staged(n):
            both = k_blk[n % STAGED // 2][:, G * (n % 2):G * (n % 2) + G, :]
            return both[:, 0:KT, :], both[:, KT:2 * KT, :]

        def staged_due(n):
            return sum(16 if ITEMS[i][2] is None else 32 for i in range(n % STAGED, n + 1, STAGED))

        def split_of(n):
            c, w = ITEMS[n][:2]
            if c is None:
                return w_cross[:, w]
            if c < 2:
                return w_in[c][:, w] if w < IN else w_out[c][:, w - IN]
            return node_t[1][:, w]

        def item_source(n):
            if n in PRODUCTS:
                return ps_proj[PRODUCTS.index(n) % 2][:].rearrange("p (k d) -> p k d", k=KT)
            return staged(n)[1]

        def scale_of(n):
            c, w = ITEMS[n][:2]
            column = CROSS_SCALES + w if c is None else (IN + OUT) * c + w
            return scales[:, column:column + 1]

        def ew(c, i):
            return scalars[:, 3 * c + i:3 * c + i + 1]

        def bcast(ap, n, m):
            return ap.rearrange("p (n o) -> p n o", o=1).to_broadcast([P, n, m])

        def rows_place(st):
            return CHAINS if st in AHEAD else st.z

        def on_all(dram, n):
            return dram.rearrange("(o n) -> o n", o=1).to_broadcast([P, n])

        @block.sync
        def _(sp):
            def load_x(it, z):
                sp.dma_start(x_in[z][:], x_v[it, z]).then_inc(x_loaded[z], 16)

            def load_ctx(it, z):
                sp.dma_start(ctx_t[z][:], ctx_v[it, z]).then_inc(ctx_loaded[z], 16)

            def stage(n):
                _, _, e, matrix = ITEMS[n]
                if e is not None:
                    sp.dma_start(staged(n)[0], a["we_t"][e]).then_inc(stage_in[n % STAGED], 16)
                sp.dma_start(staged(n)[1], matrix).then_inc(stage_in[n % STAGED], 16)

            sp.dma_start(be_col[:], a["be_col"]).then_inc(biases_in, 16)
            sp.dma_start(scalars[:, 0:3 * NODES], on_all(a["ew"], 3 * NODES)).then_inc(scalars_in, 16)
            sp.dma_start(scalars[:, 3 * NODES:4 * NODES], on_all(a["act_w"], NODES)).then_inc(scalars_in, 16)
            sp.dma_start(scalars[:, 4 * NODES:4 * NODES + 2], on_all(a["gates"], 2)).then_inc(scalars_in, 16)
            for n in range(STAGED):
                stage(n)
            for i, name in enumerate(("bo", "ln_g", "ln_b")):
                sp.dma_start(rows[:, i, :], on_all(a[name], D)).then_inc(consts_in, 16)
            sp.dma_start(b_cross[:], a["b_cross"]).then_inc(consts_in, 16)
            sp.dma_start(ident[:], a["ident"]).then_inc(consts_in, 16)
            sp.dma_start(band_f[:], a["band"]).then_inc(consts_in, 16)
            sp.dma_start(own[:], a["own"]).then_inc(consts_in, 16)
            def keep(n):
                c, w = ITEMS[n][:2]
                if c is None:
                    return
                place = a["w_in"][c, :, w] if w < IN else a["w_out"][c, :, w - IN]
                sp.wait_ge(prep_rest, n + 1)
                sp.dma_start(place, split_of(n).bitcast(F32)).then_inc(w_stored[w], 16)

            for n in range(STAGED, len(ITEMS)):
                sp.wait_ge(prep_rest, n - STAGED + 1)
                stage(n)
                keep(n - STAGED)
                if n == len(ITEMS) - 2 * STAGED:
                    load_x(0, 0)
                    load_ctx(0, 0)
            for z in range(1, CHAINS):
                load_x(0, z)
                load_ctx(0, z)
            for n in range(len(ITEMS) - STAGED, len(ITEMS)):
                keep(n)
            for w in range(IN + OUT):
                sp.wait_ge(w_stored[w], 16 * NODES)

            def load_in(c):
                sp.dma_start(w_in[c % 2][:].bitcast(F32), a["w_in"][c]).then_inc(in_loaded[c % 2], 16)

            def load_out(c):
                sp.dma_start(w_out[c % 2][:].bitcast(F32), a["w_out"][c]).then_inc(out_loaded[c % 2], 16)

            def reload_in(it, c):
                used = [st for st in PROJ if st.z == CHAINS - 1 and st.stage == c + 1 and st.kind in ("qh", "k", "v")]
                sp.wait_ge(*at("projected", it, used[-1]))
                load_in((c + 2) % NODES)

            def reload_out(it, c):
                last = c == NODES - 1
                sp.wait_ge(*at("projected", it, Step("last_out" if last else "node_out", CHAINS - 1, c + 2, 0)))
                load_out((c + 2) % NODES)

            def store(it, z):
                sp.wait_ge(result_ready, it * CHAINS + z + 1)
                sp.dma_start(out_v[it, z], result[z][:]).then_inc(stored[z], 16)

            with sp.Fori(0, ITERS - 1) as it:
                for z in range(CHAINS):
                    sp.wait_ge(x_used[z], it + 1)
                    load_x(it + 1, z)
                    sp.wait_ge(*at("ctx_split", it, Step("split", z, CROSS, 0)))
                    load_ctx(it + 1, z)
                reload_in(it, 0)
                for c in range(1, NODES):
                    reload_in(it, c)
                    reload_out(it, c - 1)
                store(it, 0)
                reload_out(it, NODES - 1)
                store(it, 1)
            it = ITERS - 1
            sp.wait_ge(x_used[0], ITERS)
            load_x(0, 0)
            sp.wait_ge(*at("ctx_split", it, Step("split", 0, CROSS, 0)))
            load_ctx(0, 0)
            for c in range(NODES - 2):
                reload_in(it, c)
                if c:
                    reload_out(it, c - 1)
            reload_out(it, NODES - 3)
            for z in range(CHAINS):
                store(it, z)
                sp.wait_ge(stored[z], 16 * ITERS)

        @block.gpsimd
        def _(pool):
            for z in range(CHAINS):
                nc.gpsimd.memset(v_pad[z][:], 0.0).then_inc(zeroed, 1)
            nc.gpsimd.memset(half_neg[:], -0.5).then_inc(zeroed, 1)
            pool.wait_ge(zeroed, 3)
            pool.wait_ge(prep_dve, 1)
            both = [P, PAIR, D]

            def step(it, st):
                z = st.z
                if st.kind == "split":
                    pool.wait_ge(*at("ctx_high", it, st))
                    nc.gpsimd.tensor_tensor(ctx_s[z][:, REST], ctx_t[z][:], ctx_s[z][:, HIGH].bitcast(F32),
                                            ALU.subtract).then_inc(sig("ctx_split", st), 1)
                elif st.kind == "moments":
                    pool.wait_ge(*at("var_ready", it, st))
                    nc.gpsimd.tensor_tensor(rstd[:, rows_place(st)], var_eps[:, rows_place(st)], half_neg[:],
                                            ALU.pow).then_inc(sig("rstd_ready", st), 1)
                elif st.kind == "normalize" and st.stage == CROSS:
                    pool.wait_ge(*at("normed", it, st))
                    nc.gpsimd.tensor_tensor(x_bias[z][:], x_in[z][:],
                                            rows[:, 0:1, :].to_broadcast(both), ALU.add).then_inc(x_used[z], 1)
                elif st.kind == "normalize" and st.stage == 1:
                    pool.wait_ge(*at("normed", it, st))
                    nc.gpsimd.tensor_tensor(x1[z][:], x1[z][:],
                                            rows[:, 2:3, :].to_broadcast(both), ALU.add).then_inc(x1_biased, 1)
                elif st.kind == "normalize":
                    pool.wait_ge(*at("normed", it, st))
                    nc.gpsimd.tensor_tensor(result[z][:], result[z][:],
                                            rows[:, 1:2, :].to_broadcast(both), ALU.mult).then_inc(pool_step, 1)
                    pool.wait_ge(pool_step, it * CHAINS + z + 1)
                    pool.wait_ge(x1_biased, it * CHAINS + CHAINS)
                    nc.gpsimd.tensor_tensor(result[z][:], result[z][:], x1[z][:],
                                            ALU.add).then_inc(result_ready, 1)
                elif st.kind == "scale":
                    u = number(st)
                    pool.wait_ge(*at("inv_ready", it, st))
                    p = probs[:, u % 3]
                    nc.gpsimd.tensor_tensor(p, p, bcast(inv_sum[:, u % 4, :], G, SEQ),
                                            ALU.mult).then_inc(sig("scaled", st), 1)

            for st in FIRST["pool"]:
                step(0, st)
            with pool.Fori(0, ITERS) as it:
                for st in ORDER["pool"]:
                    step(it + 1 if st in AHEAD else it, st)

        @block.scalar
        def _(act):
            act.wait_ge(scalars_in, 3 * 16)
            nc.scalar.activation(gates[:], scalars[:, 4 * NODES:4 * NODES + 2], ACT.Tanh).then_inc(gates_ready, 1)
            act.wait_ge(scales_ready, 1)
            for n, (c, w, e, _) in enumerate(ITEMS):
                if n in PRODUCTS:
                    act.wait_ge(prep_pe, PRODUCTS.index(n) + 1)
                    nc.scalar.activation(b_node[:, c, w], ps_score[PRODUCTS.index(n) % 2][:, 0:KT], ACT.Copy,
                                         scale=scale_of(n))
                else:
                    act.wait_ge(stage_in[n % STAGED], staged_due(n))
                if c is not None and c > 2:
                    act.wait_ge(w_stored[w], 16 * c)
                nc.scalar.activation(split_of(n)[:, HIGH], item_source(n), ACT.Copy,
                                     scale=scale_of(n)).then_inc(prep_high, 1)

            def take(it, st, bias, out):
                ps = ps_proj[bank_of(st)]
                for h in range(KT):
                    last = nc.scalar.activation(out[:, h, :], ps[:, h * TOK:(h + 1) * TOK], ACT.Identity,
                                                bias=bias[:, h:h + 1])
                last.then_inc(sig("act_took", st), 1)

            def step(it, st):
                z, c = st.z, st.stage - 1
                if st.kind in SIGNALS["act_took"]:
                    act.wait_ge(*at("projected", it, st))
                    ps = ps_proj[bank_of(st)]
                if st.kind == "turn":
                    slot = 3 if st.stage == CROSS else 0
                    nc.scalar.activation(node_t[z][:, slot, HIGH].rearrange("p k t -> p (k t)"), ps[:],
                                         ACT.Copy).then_inc(sig("act_took", st), 1)
                elif st.kind == "keys":
                    take(it, st, b_cross[:, 1], k_t[z])
                elif st.kind == "q" and st.stage == CROSS:
                    take(it, st, b_cross[:, 0], qh_t[z])
                elif st.kind == "qh":
                    act.wait_ge(*at("scored", it, Step("scores", z, st.stage - 1, UNITS_OF[st.stage - 1] - 1)))
                    take(it, st, b_node[:, c, WQH], qh_t[z])
                elif st.kind == "node_out":
                    take(it, st, b_node[:, c - 1, WQ], node_t[z][:, SLOT[c - 1], HIGH])
                elif st.kind == "last_out":
                    take(it, st, b_node[:, c - 1, WQ], qh_t[z])
                elif st.kind == "v" and st.stage == CROSS:
                    src = ps[:].rearrange("p (g e d) -> p g e d", e=2, d=A_DH)
                    nc.scalar.activation(v_pad[z][:, :, 0:A_DH], src[:, :, 0, :], ACT.Copy)
                    nc.scalar.activation(v_pad[z][:, :, 48:64], src[:, :, 1, :],
                                         ACT.Copy).then_inc(sig("act_took", st), 1)
                elif st.kind == "v":
                    if st.stage >= 2:
                        act.wait_ge(*at("mixed", it, Step("mix", z, st.stage - 1, UNITS_OF[st.stage - 1] - 1)))
                    nc.scalar.activation(v_row[z][:].rearrange("p b d -> p (b d)"), ps[:],
                                         ACT.Copy).then_inc(sig("act_took", st), 1)
                elif st.kind == "scores":
                    u = number(st)
                    act.wait_ge(*at("max_ready", it, st))
                    if u >= 3:
                        act.wait_ge(*at("turned_p", it, of_unit("turn_p", u - 3)))
                    for j in range(G):
                        last = nc.scalar.activation(
                            probs[:, u % 3, j, :], ps_score[u % 2][:, j * SEQ:(j + 1) * SEQ], ACT.Exp,
                            bias=neg_max[:, u % 4, j:j + 1], accum_out=row_sum[:, u % 4, j:j + 1])
                    last.then_inc(sig("exp_done", st), 1)
                elif st.kind == "mix" and OUT_OF[st][2]:
                    act.wait_ge(*at("mixed", it, st))
                    half = unit_of(st)[1]
                    bias = b_cross[:, 2] if st.stage == CROSS else b_node[:, c, WV]
                    nc.scalar.activation(o_t[z][:, HIGH, half, :], ps_out[OUT_OF[st][0] % 2][:, 0:TOK], ACT.Identity,
                                         bias=bias[:, half:half + 1]).then_inc(out_high, 1)

            for st in FIRST["act"]:
                step(0, st)
            with act.Fori(0, ITERS) as it:
                for st in ORDER["act"]:
                    step(it + 1 if st in AHEAD else it, st)

        @block.vector
        def _(dve):
            dve.wait_ge(scalars_in, 3 * 16)
            dve.wait_ge(gates_ready, 1)
            dve.wait_ge(biases_in, 16)
            for c in range(NODES):
                nc.vector.tensor_scalar(b_node[:, c, WQ], be_col[:, WIRES[c]["eq"]], ew(c, 0), None, ALU.mult)
            by_node = scales[:, 0:CROSS_SCALES].rearrange("p (c w) -> p c w", c=NODES)
            edges = scalars[:, 0:3 * NODES].rearrange("p (c w) -> p c w", c=NODES)
            nc.vector.memset(scales[:, CROSS_SCALES + AQ:CROSS_SCALES + AQ + 1], A_DH ** -0.5)
            nc.vector.memset(scales[:, CROSS_SCALES + AK:CROSS_SCALES + AV + 1], 1.0)
            nc.vector.tensor_copy(scales[:, CROSS_SCALES + AO:CROSS_SCALES + AO + 1], gates[:, 0:1])
            nc.vector.tensor_scalar(by_node[:, :, WQH], edges[:, :, 0], N_DH ** -0.5, None, ALU.mult)
            nc.vector.tensor_copy(by_node[:, :, WK:WV + 1], edges[:, :, 1:3])
            nc.vector.tensor_copy(by_node[:, :, WQ], edges[:, :, 0])
            nc.vector.tensor_copy(by_node[:, :, WO], scalars[:, 3 * NODES:4 * NODES]).then_inc(scales_ready, 1)
            dve.wait_ge(scales_ready, 1)
            for n in range(len(ITEMS)):
                if n == IN + OUT:
                    dve.wait_ge(consts_in, 7 * 16)
                    nc.vector.tensor_copy(ident_r[:], ident[:])
                    nc.vector.tensor_copy(band_r[:],
                                          band_f[:].rearrange("p (o k) -> p o k", o=1).to_broadcast([P, G, P]))
                    nc.vector.tensor_scalar(rows[:, 0, :], rows[:, 0, :], gates[:, 0:1], None, ALU.mult)
                    nc.vector.tensor_scalar(rows[:, 1:3, :], rows[:, 1:3, :], gates[:, 1:2], None, ALU.mult)
                    nc.vector.tensor_scalar(b_cross[:, 0], b_cross[:, 0], A_DH ** -0.5, None, ALU.mult)\
                        .then_inc(prep_dve, 1)
                dve.wait_ge(prep_high, n + 1)
                nc.vector.scalar_tensor_tensor(
                    out=split_of(n)[:, REST], in0=item_source(n), scalar=scale_of(n),
                    in1=split_of(n)[:, HIGH].bitcast(F32), op0=ALU.mult, op1=ALU.subtract).then_inc(prep_rest, 1)

            def rows_of(st):
                z = st.z
                if st.stage == CROSS:
                    return [x_in[z][:, b, :] for b in range(PAIR)], EPS_PRE
                if st.stage == 1:
                    return [x1[z][:, b, :] for b in range(PAIR)], EPS_PRE
                ps = ps_proj[bank_of(Step("turn_back", z, STAGES, 0))]
                return [ps[:, b * D:(b + 1) * D] for b in range(PAIR)], EPS_OUT

            def step(it, st):
                z, c = st.z, st.stage - 1
                if st.kind in SIGNALS["dve_took"]:
                    dve.wait_ge(*at("projected", it, st))
                    ps = ps_proj[bank_of(st)]
                if st.kind == "split":
                    dve.wait_ge(ctx_loaded[z], it * 16 + 16)
                    nc.vector.tensor_copy(ctx_s[z][:, HIGH], ctx_t[z][:]).then_inc(sig("ctx_high", st), 1)
                elif st.kind == "turn":
                    dve.wait_ge(*at("act_took", it, st))
                    parts = node_t[z][:, 3 if st.stage == CROSS else 0]
                    nc.vector.tensor_tensor(parts[:, REST], ps[:].rearrange("p (k t) -> p k t", k=KT),
                                            parts[:, HIGH].bitcast(F32), ALU.subtract)\
                        .then_inc(sig("dve_took", st), 1)
                elif st.kind == "node_out":
                    dve.wait_ge(*at("act_took", it, st))
                    parts = node_t[z][:, SLOT[c - 1]]
                    for half in range(KT):
                        last = nc.vector.scalar_tensor_tensor(
                            out=parts[:, REST, half, :], in0=ps[:, half * TOK:(half + 1) * TOK],
                            scalar=b_node[:, c - 1, WQ, half:half + 1], in1=parts[:, HIGH, half, :].bitcast(F32),
                            op0=ALU.add, op1=ALU.subtract)
                    last.then_inc(sig("dve_took", st), 1)
                elif st.kind == "out_rest":
                    half, n = st.part, out_due(it, z, st.stage, st.part)
                    dve.wait_ge(out_high, n)
                    bias = b_cross[:, 2] if st.stage == CROSS else b_node[:, c, WV]
                    nc.vector.scalar_tensor_tensor(
                        out=o_t[z][:, REST, half, :], in0=ps_out[out_due(0, z, st.stage, half) % 2 ^ 1][:, 0:TOK],
                        scalar=bias[:, half:half + 1], in1=o_t[z][:, HIGH, half, :].bitcast(F32),
                        op0=ALU.add, op1=ALU.subtract).then_inc(out_taken, 1)
                elif st.kind == "moments":
                    if st.stage == CROSS:
                        dve.wait_ge(x_loaded[z], it * 16 + 16)
                    elif st.stage == 1:
                        dve.wait_ge(*at("dve_took", it, Step("cross_out", z, 1, 0)))
                    else:
                        dve.wait_ge(*at("projected", it, Step("turn_back", z, STAGES, 0)))
                    rows_in, eps = rows_of(st)
                    own_order = dve_step[st in AHEAD]
                    n = 2 * (due("var_ready", it, st) - 1)
                    for b in range(PAIR):
                        last = nc.vector.bn_stats(stats[:, rows_place(st), b, :], rows_in[b])
                    last.then_inc(own_order, 1)
                    dve.wait_ge(own_order, n + 1)
                    nc.vector.memset(idle[:], 0.0)
                    for b in range(PAIR):
                        last = nc.vector.bn_aggr(moments[:, rows_place(st), b, :], stats[:, rows_place(st), b, :])
                    last.then_inc(own_order, 1)
                    dve.wait_ge(own_order, n + 2)
                    nc.vector.tensor_scalar(var_eps[:, rows_place(st)], moments[:, rows_place(st), :, 1], eps, None,
                                            ALU.add).then_inc(sig("var_ready", st), 1)
                elif st.kind == "normalize":
                    rows_in, _ = rows_of(st)
                    out = result[z] if st.stage == STAGES else normed_x[z]
                    if st.stage == STAGES:
                        dve.wait_ge(stored[z], it * 16)
                    dve.wait_ge(*at("rstd_ready", it, Step("moments", z, st.stage, 0)))
                    for b in range(PAIR):
                        last = nc.vector.tensor_scalar(out[:, b, :], rows_in[b], moments[:, rows_place(st), b, 0:1],
                                                       rstd[:, rows_place(st), b:b + 1], ALU.subtract, ALU.mult)
                    last.then_inc(sig("normed", st), 1)
                elif st.kind == "cross_out":
                    dve.wait_ge(x_used[z], it + 1)
                    dve.wait_ge(result_ready, it * CHAINS)
                    nc.vector.tensor_tensor(x1[z][:].rearrange("p b d -> p (b d)"), ps[:],
                                            x_bias[z][:].rearrange("p b d -> p (b d)"),
                                            ALU.add).then_inc(sig("dve_took", st), 1)
                elif st.kind == "k":
                    half = st.part
                    dve.wait_ge(*at("scored", it, Step("scores", z, st.stage - 1, LAST_WITH[st.stage - 1][half])))
                    keys = ps[:, 0:TOK].rearrange("p (o t) -> p o t", o=1).to_broadcast([P, G, TOK])
                    nc.vector.scalar_tensor_tensor(
                        out=k_blk[z][:, G * half:G * half + G, :], in0=keys, scalar=b_node[:, c, WK, half:half + 1],
                        in1=bcast(own[:, 8:12], G, TOK), op0=ALU.add, op1=ALU.mult).then_inc(sig("dve_took", st), 1)
                elif st.kind == "quad":
                    half, place = st.part // 2, G * (st.part % 2)
                    dve.wait_ge(*at("act_took", it, Step("keys", z, CROSS, 0)))
                    if st.part >= 2:
                        dve.wait_ge(*at("scored", it, Step("scores", z, CROSS, 2 * (st.part - 2) + 1)))
                    nc.vector.tensor_tensor(
                        k_blk[z][:, place:place + G, :], k_t[z][:, half:half + 1, :].to_broadcast([P, G, TOK]),
                        bcast(own[:, place:place + G], G, TOK), ALU.mult).then_inc(sig("quad_ready", st), 1)
                elif st.kind == "scores":
                    u = number(st)
                    dve.wait_ge(*at("scored", it, st))
                    nc.vector.tensor_reduce(neg_max[:, u % 4, :],
                                            ps_score[u % 2][:].rearrange("p (h k) -> p h k", h=G),
                                            AX_X, ALU.max, negate=True).then_inc(sig("max_ready", st), 1)
                elif st.kind == "scale":
                    u = number(st)
                    dve.wait_ge(*at("exp_done", it, Step("scores", z, st.stage, st.part)))
                    nc.vector.reciprocal(inv_sum[:, u % 4, :], row_sum[:, u % 4, :]).then_inc(sig("inv_ready", st), 1)
                elif st.kind == "turn_p":
                    u = number(st)
                    dve.wait_ge(*at("turned_p", it, st))
                    if u >= 2:
                        dve.wait_ge(*at("mixed", it, of_unit("mix", u - 2)))
                    nc.vector.tensor_copy(probs_t[:, u % 2].rearrange("p h q -> p (h q)"),
                                          ps_turn[u % 2][:]).then_inc(sig("pt_ready", st), 1)

            for st in FIRST["dve"]:
                step(0, st)
            with dve.Fori(0, ITERS) as it:
                for st in ORDER["dve"]:
                    step(it + 1 if st in AHEAD else it, st)

        @block.tensor
        def _(pe):
            PASSES = ((HIGH, HIGH), (HIGH, REST), (REST, HIGH))

            def project(ps, col, w, src, half, start=True, stop=True):
                terms = [(k, i, j) for k in range(KT) for i, j in PASSES]
                for n, (k, i, j) in enumerate(terms):
                    last = nc.tensor.matmul(ps[:, col:col + TOK], w[:, i, k, half * P:(half + 1) * P], src[:, j, k, :],
                                            start=(start and n == 0), stop=(stop and n == len(terms) - 1))
                return last

            def project_rows(ps, w, src):
                terms = [(k, i, j) for k in range(KT) for i, j in PASSES]
                for b in range(PAIR):
                    for n, (k, i, j) in enumerate(terms):
                        last = nc.tensor.matmul(ps[:, b * D:(b + 1) * D], src[:, i, k, b * SEQ:(b + 1) * SEQ],
                                                w[:, j, k, :], start=(n == 0), stop=(n == len(terms) - 1))
                return last

            pe.wait_ge(biases_in, 16)
            for m, n in enumerate(PRODUCTS):
                e = ITEMS[n][2]
                pe.wait_ge(stage_in[n % STAGED], staged_due(n))
                if m >= 2:
                    pe.wait_ge(prep_rest, PRODUCTS[m - 2] + 1)
                lhs, rhs = staged(n)
                for h in range(KT):
                    for k in range(KT):
                        nc.tensor.matmul(ps_score[m % 2][:, h:h + 1], rhs[:, k, h * P:(h + 1) * P],
                                         be_col[:, e, k:k + 1], start=(k == 0), stop=(k == KT - 1))
                for h in range(KT):
                    for k in range(KT):
                        last = nc.tensor.matmul(ps_proj[m % 2][:, h * D:(h + 1) * D], lhs[:, k, h * P:(h + 1) * P],
                                                rhs[:, k, :], start=(k == 0), stop=(k == KT - 1))
                last.then_inc(prep_pe, 1)
            pe.wait_ge(prep_rest, PRODUCTS[-1] + 1)
            pe.wait_ge(prep_dve, 1)
            pe.wait_ge(zeroed, 3)

            def taken_by(st):
                return "dve_took" if st.kind in SIGNALS["dve_took"] else "act_took"

            def bank_for(it, st):
                before = PROJ[PROJ.index(st) - 2]
                shift = (before in AHEAD) - (st in AHEAD) - (PROJ.index(st) < 2)
                if before.kind == "turn_back":
                    pe.wait_ge(*at("normed", it, Step("normalize", before.z, STAGES, 0), shift))
                else:
                    pe.wait_ge(*at(taken_by(before), it, before, shift))
                return ps_proj[bank_of(st)]

            def bank_in_turn(n):
                st, before = ahead_proj[n], ahead_proj[n - 1]
                if n:
                    pe.wait_ge(*at(taken_by(before), 0, before))
                return ps_proj[bank_of(st)]

            ahead_proj = [st for st in FIRST["pe"] if st.kind in SIGNALS["projected"]]

            def node_ready(it, z, n):
                if n == -1:
                    pe.wait_ge(*at("dve_took", it, Step("turn", z, 1, 0)))
                else:
                    pe.wait_ge(*at("dve_took", it, Step("node_out", z, n + 2, 0)))
                return node_t[z][:, SLOT[n]]

            def weight(it, c, w):
                loaded, tile, first = (in_loaded, w_in, 0) if w < IN else (out_loaded, w_out, IN)
                pe.wait_ge(loaded[c % 2], it * (16 * NODES // 2) + 16 * (c // 2))
                return tile[c % 2][:, w - first]

            def step(it, st, before_loop=False):
                z, c = st.z, st.stage - 1
                if st.kind in SIGNALS["projected"]:
                    ps = bank_in_turn(ahead_proj.index(st)) if before_loop else bank_for(it, st)
                if st.kind == "turn":
                    pe.wait_ge(*at("normed", it, Step("normalize", z, st.stage, 0)))
                    for k in range(KT):
                        for b in range(PAIR):
                            last = nc.tensor.transpose(ps[:, (k * PAIR + b) * P:(k * PAIR + b + 1) * P],
                                                       normed_x[z][:, b, k * P:(k + 1) * P], ident[:])
                    last.then_inc(sig("projected", st), 1)
                elif st.kind == "turn_back":
                    pe.wait_ge(*at("act_took", it, Step("last_out", z, st.stage, 0)))
                    for b in range(PAIR):
                        for k in range(KT):
                            last = nc.tensor.transpose(ps[:, (b * KT + k) * P:(b * KT + k + 1) * P],
                                                       qh_t[z][:, k, b * SEQ:(b + 1) * SEQ], ident[:])
                    last.then_inc(sig("projected", st), 1)
                elif st.kind == "keys":
                    pe.wait_ge(*at("ctx_split", it, Step("split", z, CROSS, 0)))
                    project(ps, 0, w_cross[:, AK], ctx_s[z], 0)
                    project(ps, TOK, w_cross[:, AK], ctx_s[z], 1).then_inc(sig("projected", st), 1)
                elif st.kind == "k":
                    project(ps, 0, weight(it, c, WK), node_ready(it, z, WIRES[c]["k"]), st.part)\
                        .then_inc(sig("projected", st), 1)
                elif st.kind == "v" and st.stage == CROSS:
                    pe.wait_ge(*at("ctx_split", it, Step("split", z, CROSS, 0)))
                    project_rows(ps, w_cross[:, AV], ctx_s[z]).then_inc(sig("projected", st), 1)
                elif st.kind == "v":
                    project_rows(ps, weight(it, c, WV), node_ready(it, z, WIRES[c]["v"]))\
                        .then_inc(sig("projected", st), 1)
                elif st.kind == "q":
                    pe.wait_ge(*at("dve_took", it, Step("turn", z, 0, 0)))
                    project(ps, 0, w_cross[:, AQ], node_t[z][:, 3], 0)
                    project(ps, TOK, w_cross[:, AQ], node_t[z][:, 3], 1).then_inc(sig("projected", st), 1)
                elif st.kind == "qh":
                    source = node_ready(it, z, WIRES[c]["q"])
                    w = weight(it, c, WQH)
                    project(ps, 0, w, source, 0)
                    project(ps, TOK, w, source, 1).then_inc(sig("projected", st), 1)
                elif st.kind == "cross_out":
                    pe.wait_ge(out_taken, out_due(it, z, CROSS, 1))
                    project_rows(ps, w_cross[:, AO], o_t[z]).then_inc(sig("projected", st), 1)
                elif st.kind in ("node_out", "last_out"):
                    before = node_ready(it, z, WIRES[c - 1]["q"])
                    edge, mixed = weight(it, c - 1, WQ), weight(it, c - 1, WO)
                    project(ps, 0, edge, before, 0, stop=False)
                    pe.wait_ge(out_taken, out_due(it, z, st.stage - 1, 1))
                    project(ps, 0, mixed, o_t[z], 0, start=False)
                    project(ps, TOK, edge, before, 1, stop=False)
                    project(ps, TOK, mixed, o_t[z], 1, start=False).then_inc(sig("projected", st), 1)
                elif st.kind == "scores":
                    u = number(st)
                    b, half, place = unit_of(st)
                    if u < 2:
                        pe.wait_ge(of_body["exp_done"], it * TOTAL["exp_done", False])
                    else:
                        pe.wait_ge(*at("exp_done", it, of_unit("scores", u - 2)))
                    if st.stage == CROSS:
                        pe.wait_ge(*at("act_took", it, Step("q", z, CROSS, 0)))
                        pe.wait_ge(*at("quad_ready", it, Step("quad", z, CROSS, st.part // 2)))
                        nc.tensor.matmul(ps_score[u % 2][:], ident_r[:], band_r[:].rearrange("p h k -> p (h k)"),
                                         start=True, stop=False)
                    else:
                        pe.wait_ge(*at("act_took", it, Step("qh", z, st.stage, 0)))
                        pe.wait_ge(*at("dve_took", it, Step("k", z, st.stage, half)))
                    nc.tensor.matmul(ps_score[u % 2][:].rearrange("p (h k) -> p h k", h=G),
                                     qh_t[z][:, half, b * SEQ:(b + 1) * SEQ],
                                     k_blk[z][:, place:place + G, b * SEQ:(b + 1) * SEQ],
                                     start=(st.stage != CROSS), stop=True).then_inc(sig("scored", st), 1)
                elif st.kind == "turn_p":
                    u = number(st)
                    pe.wait_ge(*at("scaled", it, Step("scale", z, st.stage, st.part)))
                    if u >= 2:
                        pe.wait_ge(*at("pt_ready", it, of_unit("turn_p", u - 2)))
                    for j in range(G):
                        last = nc.tensor.transpose(ps_turn[u % 2][:, j * P:(j + 1) * P], probs[:, u % 3, j, :],
                                                   ident[:])
                    last.then_inc(sig("turned_p", st), 1)
                elif st.kind == "mix":
                    u = number(st)
                    b, half, _ = unit_of(st)
                    n, first, _ = OUT_OF[st]
                    if first and n < 2:
                        pe.wait_ge(out_taken, it * OUTS)
                    elif first:
                        pe.wait_ge(out_taken, it * OUTS + n - 1)
                    pe.wait_ge(*at("act_took", it, Step("v", z, st.stage, 0)))
                    pe.wait_ge(*at("pt_ready", it, Step("turn_p", z, st.stage, st.part)))
                    for j in (0, 2, 1, 3) if st.stage == CROSS else range(G):
                        if st.stage == CROSS:
                            head = G * (st.part // 2) + j
                            row = 32 * (head % 8 // 2)
                            v = v_pad[z][:, (A_HEADS // 2) * b + head // 2, 32 * (j % 2):32 * (j % 2) + 32]
                            start, stop = j % 2 == 0, j % 2 == 1
                        else:
                            row = 32 * j
                            v = v_row[z][:, b, half * P + row:half * P + row + 32]
                            start = stop = True
                        last = nc.tensor.matmul(ps_out[n % 2][row:row + 32, b * SEQ:(b + 1) * SEQ], v,
                                                probs_t[:, u % 2, j, :], start=start, stop=stop)
                    last.then_inc(sig("mixed", st), 1)

            for st in FIRST["pe"]:
                step(0, st, True)
            pe.wait_ge(prep_rest, len(ITEMS))
            for w in range(IN + OUT):
                pe.wait_ge(w_stored[w], 16 * NODES)
            with pe.Fori(0, ITERS) as it:
                for st in ORDER["pe"]:
                    step(it + 1 if st in AHEAD else it, st)


def kernel(**inputs):
    import concourse.bacc as bacc
    from concourse.bass_utils import run_bass_kernel_spmd as run

    def arr(name):
        return np.asarray(inputs[name])

    def split_rows(w):
        w = w.reshape(w.shape[:-2] + (KT, P, w.shape[-1]))
        return np.ascontiguousarray(np.swapaxes(w, -3, -2))

    def cols(b):
        return np.ascontiguousarray(b.reshape(-1, KT, P).transpose(2, 0, 1))

    ctx = arr("ctx_1024").reshape(ITERS, CHAINS, TOK, D).transpose(0, 1, 3, 2)
    row = np.arange(P)
    own = np.concatenate([row[:, None] // A_DH == np.arange(8), row[:, None] // N_DH == np.arange(4)], 1)
    arrays = {
        "x": arr("x"),
        "ctx_t": split_rows(ctx),
        "w_cross": split_rows(np.stack([arr(f"L0_xattn_W{n}").T for n in "qkvo"])),
        "b_cross": cols(np.stack([arr(f"L0_xattn_b{n}") for n in "qkv"])),
        "bo": arr("L0_xattn_bo"),
        "ln_g": arr("L0_ffn_ln_g"),
        "ln_b": arr("L0_ffn_ln_b"),
        "ew": arr("L0_ffn_ew").reshape(-1),
        "act_w": arr("L0_ffn_act_w"),
        "gates": np.concatenate([arr("g_xattn"), arr("g_ffn")]),
        "we": split_rows(arr("L0_ffn_We")),
        "we_t": split_rows(arr("L0_ffn_We").transpose(0, 2, 1)),
        "be_col": cols(arr("L0_ffn_be")),
        "wq": split_rows(arr("L0_ffn_Wq")),
        "wk": split_rows(arr("L0_ffn_Wk")),
        "wv": split_rows(arr("L0_ffn_Wv")),
        "wo": split_rows(arr("L0_ffn_Wo")),
        "ident": np.eye(P, dtype=np.float32),
        "band": np.where(abs(row[:, None] - row[None, :]) <= WINDOW // 2, 0.0, MASKED).astype(np.float32),
        "own": own.astype(np.float32),
    }
    nc = bacc.Bacc("TRN2", target_bir_lowering=False, num_devices=1)
    aps = {n: nc.dram_tensor(f"{n}_dram", v.shape, mybir.dt.from_np(v.dtype), kind="ExternalInput").ap()
           for n, v in arrays.items()}
    for name, n in (("w_in", IN), ("w_out", OUT)):
        aps[name] = nc.dram_tensor(f"{name}_dram", (NODES, P, n, 2, KT, D), F32, kind="Internal").ap()
    aps["out"] = nc.dram_tensor("out_dram", (BATCH, SEQ, D), F32, kind="ExternalOutput").ap()
    build(nc, aps)
    fed = {f"{n}_dram": v for n, v in arrays.items()}
    return run(nc, [fed], core_ids=[0]).results[0]["out_dram"]
```
